# Optimizing a Trainium2 kernel written in Bass

```python
import numpy as np
import jax
import jax.numpy as jnp

def _softmax(x, axis=-1):
    return jax.nn.softmax(x, axis=axis)

def _gelu(x):
    return jax.nn.gelu(x, approximate=True)

def _silu(x):
    return jax.nn.silu(x)

def _sigmoid(x):
    return jax.nn.sigmoid(x)

def _layernorm(x, axis=-1, eps=1e-05):
    m = jnp.mean(x, axis=axis, keepdims=True)
    v = jnp.var(x, axis=axis, keepdims=True)
    return (x - m) / jnp.sqrt(v + eps)

def _scatter_add(tgt, idx, src, axis=0):
    return tgt.at[idx].add(src)

def _segment_sum(src, seg, n):
    return jax.ops.segment_sum(src, seg, n)
kernel_name = 'mk_adj_resnorm_d2_adj_r2_87d675'

def setup_inputs(seed: int=0):
    np.random.seed(seed)
    _w = jnp.asarray

    def _rec_inputs():
        import jax
        import jax.numpy as jnp
        _gk = jax.random.key(seed)
        x = -0.0005207 + 1.001 * jax.random.normal(jax.random.fold_in(_gk, 1), (8, 1024, 128), jnp.float32)
        _a = jax.random.bernoulli(jax.random.fold_in(_gk, 2), 0.0078125, (1024, 1024))
        _a = jnp.logical_or(_a, jnp.swapaxes(_a, -1, -2))
        _a = jnp.logical_or(_a, jnp.eye(1024, dtype=bool))
        adj = _a.astype(jnp.int32)
        return (x, adj)
    x, adj = _rec_inputs()

    def _L0_gnn_setup():
        import jax, jax.numpy as jnp
        import numpy as np
        import math
        CHUNK = 128
        NUM_HEADS = 4
        EPS = 1e-05
        key = jax.random.key(seed)
        ks = jax.random.split(key, 12)
        B, N, F = (4, 1024, 128)
        x = jax.random.normal(ks[0], (B, N, F), dtype=jnp.float32)
        adj_matrix = jax.random.randint(ks[1], (N, N), 0, 2, dtype=jnp.int32)
        s = 1.0 / math.sqrt(F)
        Wq = jax.random.normal(ks[2], (F, F), dtype=jnp.float32) * s
        bq = jnp.zeros((F,), dtype=jnp.float32)
        Wk = jax.random.normal(ks[3], (F, F), dtype=jnp.float32) * s
        bk = jnp.zeros((F,), dtype=jnp.float32)
        Wv = jax.random.normal(ks[4], (F, F), dtype=jnp.float32) * s
        bv = jnp.zeros((F,), dtype=jnp.float32)
        Wo = jax.random.normal(ks[5], (F, F), dtype=jnp.float32) * s
        bo = jnp.zeros((F,), dtype=jnp.float32)
        gamma = jnp.ones((F,), dtype=jnp.float32)
        beta = jnp.zeros((F,), dtype=jnp.float32)
        return {'x': x, 'adj_matrix': adj_matrix, 'Wq': Wq, 'bq': bq, 'Wk': Wk, 'bk': bk, 'Wv': Wv, 'bv': bv, 'Wo': Wo, 'bo': bo, 'gamma': gamma, 'beta': beta}
    _L0_gnn_all = _L0_gnn_setup()
    _L0_gnn_in = {k: v for k, v in _L0_gnn_all.items() if k in ('Wq', 'bq', 'Wk', 'bk', 'Wv', 'bv', 'Wo', 'bo', 'gamma', 'beta')}
    del _L0_gnn_all

    def _L1_gnn_setup():
        import jax, jax.numpy as jnp
        import numpy as np
        ALPHA = 0.2
        key = jax.random.key(seed)
        k1, k2, k3, k4 = jax.random.split(key, 4)
        B, N, Din, Dout = (8, 1024, 128, 128)
        h = jax.random.normal(k1, (B, N, Din), dtype=jnp.float32)
        adj = jax.random.randint(k2, (N, N), 0, 2, dtype=jnp.int32)
        w_bound = float(np.sqrt(6.0 / (Din + Dout)))
        a_bound = float(np.sqrt(6.0 / (2 * Dout + 1)))
        W = jax.random.uniform(k3, (Din, Dout), dtype=jnp.float32, minval=-w_bound, maxval=w_bound)
        a = jax.random.uniform(k4, (2 * Dout, 1), dtype=jnp.float32, minval=-a_bound, maxval=a_bound)
        return {'h': h, 'adj': adj, 'W': W, 'a': a}
    _L1_gnn_all = _L1_gnn_setup()
    _L1_gnn_in = {k: v for k, v in _L1_gnn_all.items() if k in ('W', 'a')}
    del _L1_gnn_all
    return {'x': x, 'adj': adj, 'L0_gnn_Wq': _L0_gnn_in['Wq'], 'L0_gnn_bq': _L0_gnn_in['bq'], 'L0_gnn_Wk': _L0_gnn_in['Wk'], 'L0_gnn_bk': _L0_gnn_in['bk'], 'L0_gnn_Wv': _L0_gnn_in['Wv'], 'L0_gnn_bv': _L0_gnn_in['bv'], 'L0_gnn_Wo': _L0_gnn_in['Wo'], 'L0_gnn_bo': _L0_gnn_in['bo'], 'L0_gnn_gamma': _L0_gnn_in['gamma'], 'L0_gnn_beta': _L0_gnn_in['beta'], 'L1_gnn_W': _L1_gnn_in['W'], 'L1_gnn_a': _L1_gnn_in['a']}

def reference(x, adj, L0_gnn_Wq, L0_gnn_bq, L0_gnn_Wk, L0_gnn_bk, L0_gnn_Wv, L0_gnn_bv, L0_gnn_Wo, L0_gnn_bo, L0_gnn_gamma, L0_gnn_beta, L1_gnn_W, L1_gnn_a):
    import jax
    import jax.numpy as jnp

    def _L0_gnn_ref(x, adj_matrix, Wq, bq, Wk, bk, Wv, bv, Wo, bo, gamma, beta):
        import jax, jax.numpy as jnp
        import numpy as np
        import math
        CHUNK = 128
        NUM_HEADS = 4
        EPS = 1e-05
        B, N, Fin = x.shape
        H = NUM_HEADS
        Dout = Wq.shape[0]
        Dh = Dout // H
        Nc = N // CHUNK
        q = (x @ Wq.T + bq).reshape(B, N, H, Dh).transpose(0, 2, 1, 3)
        k = (x @ Wk.T + bk).reshape(B, N, H, Dh).transpose(0, 2, 1, 3)
        v = (x @ Wv.T + bv).reshape(B, N, H, Dh).transpose(0, 2, 1, 3)
        kc = k.reshape(B, H, Nc, CHUNK, Dh)
        vc = v.reshape(B, H, Nc, CHUNK, Dh)
        scores = jnp.einsum('bhnd,bhjcd->bhnjc', q, kc) / jnp.sqrt(jnp.asarray(Dh, dtype=q.dtype))
        scores = jnp.clip(scores, -10.0, 10.0)
        mask = adj_matrix.reshape(N, Nc, CHUNK)[None, None]
        scores = jnp.where(mask == 0, jnp.asarray(-10.0, scores.dtype), scores)
        attn = jax.nn.softmax(scores, axis=-1)
        ctx = jnp.einsum('bhnjc,bhjcd->bhnd', attn, vc)
        ctx = ctx.transpose(0, 2, 1, 3).reshape(B, N, Dout)
        out = ctx @ Wo.T + bo
        out = out + x
        mu = jnp.mean(out, axis=-1, keepdims=True)
        var = jnp.mean(jnp.square(out - mu), axis=-1, keepdims=True)
        out = (out - mu) * jax.lax.rsqrt(var + EPS) * gamma + beta
        return out

    def _L1_gnn_ref(h, adj, W, a):
        import jax, jax.numpy as jnp
        import numpy as np
        ALPHA = 0.2
        Wh = jnp.matmul(h, W)
        D = W.shape[1]
        e_src = jnp.matmul(Wh, a[:D])
        e_dst = jnp.matmul(Wh, a[D:])
        e = e_src + jnp.swapaxes(e_dst, 1, 2)
        e = jnp.where(e > 0, e, ALPHA * e)
        mask = (adj > 0)[None, :, :]
        e = jnp.where(mask, e, -jnp.inf)
        alpha_w = jax.nn.softmax(e, axis=-1)
        h_prime = jnp.matmul(alpha_w, Wh)
        return jax.nn.elu(h_prime)
    x = _layernorm(x + _L0_gnn_ref(x, adj, L0_gnn_Wq, L0_gnn_bq, L0_gnn_Wk, L0_gnn_bk, L0_gnn_Wv, L0_gnn_bv, L0_gnn_Wo, L0_gnn_bo, L0_gnn_gamma, L0_gnn_beta), axis=-1)
    x = _layernorm(x + _L1_gnn_ref(x, adj, L1_gnn_W, L1_gnn_a), axis=-1)
    return x

_drawn_inputs = setup_inputs


def setup_inputs(seed=0):
    import zlib

    import numpy as np

    out = dict(_drawn_inputs(seed))
    spreads = {'L0_gnn_bq': (0.0, 0.389),
     'L0_gnn_bk': (0.0, 2.0),
     'L0_gnn_bv': (0.0, 0.1),
     'L0_gnn_bo': (0.0, 0.269),
     'L0_gnn_gamma': (1.0, 0.2),
     'L0_gnn_beta': (0.0, 0.1)}
    factors = {}
    for name, (base, spread) in spreads.items():
        noise = np.random.default_rng([zlib.crc32(name.encode()), seed]).standard_normal(out[name].shape)
        drawn = base * np.exp(spread * noise) if base else spread * noise
        out[name] = jnp.asarray(drawn.astype(out[name].dtype))
    for name, factor in factors.items():
        out[name] = (out[name] * factor).astype(out[name].dtype)
    return out
```

```python
import math
from contextlib import ExitStack

import numpy as np

import concourse.bass as bass
from concourse import mybir

F32 = mybir.dt.float32
F32R = mybir.dt.float32r
BF16 = mybir.dt.bfloat16
U8 = mybir.dt.uint8
I32 = mybir.dt.int32
ALU = mybir.AluOpType
ACT = mybir.ActivationFunctionType
AX = mybir.AxisListType

P = 128
HEADS = 4
SCORE_CLIP = 10.0
NEG_SLOPE = 0.2
LN_EPS = 1e-5
NEG_BIG = -1e30


def build(nc, x, adj, Wq, bq, Wk, bk, Wv, bv, Wo, bo, gamma, beta, W1, a1, out):
    B, N, F = x.shape
    assert F == P and N % P == 0
    NT = N // P
    DH = F // HEADS
    HALF = 512
    NH = N // HALF
    Q = 4
    NQ = N // Q
    assert NT * Q == DH and NT == 8
    SCALE = 1.0 / math.sqrt(DH)
    LO = float(np.exp(np.float32(-SCORE_CLIP)))
    HI = float(np.exp(np.float32(SCORE_CLIP)))
    E_SLOTS = 3
    P_SLOTS = 2 * HEADS
    STACKS = 8 * HEADS

    with ExitStack() as ctx:
        def sb(name, shape, dt=F32):
            return ctx.enter_context(nc.sbuf_tensor(name, shape, dt))

        def sem(name):
            return ctx.enter_context(nc.semaphore(name))

        ident = sb("ident", [P, P])
        ident_bf = sb("ident_bf", [P, P], BF16)
        ones32 = sb("ones32", [P, DH])
        one_hot = sb("one_hot", [P, 2 * DH - 1])
        sel = sb("sel", [P, NT * Q, P], BF16)
        quad_first = sb("quad_first", [P, 1])
        w_nat = sb("w_nat", [P, 5, F])
        w_t = sb("w_t", [P, 5, F])
        bias_col = sb("bias_col", [P, 2])
        rows = sb("rows", [P, 4, F])
        a_sb = sb("a_sb", [P, 2])
        wa = sb("wa", [P, 2])
        eps_col = sb("eps_col", [P, 1])
        clip_t = sb("clip_t", [P, NT, N])
        keep_t = sb("keep_t", [P, NT, N], U8)
        bias_n = sb("bias_n", [P, NT, N], BF16)
        x_sb = sb("x_sb", [P, NT, F])
        xT = sb("xT", [P, N])
        k_st = sb("k_st", [P, HEADS, N], F32R)
        q_st = sb("q_st", [P, HEADS, N], F32R)
        v_sb = sb("v_sb", [P, NT, F])
        e_sb = sb("e_sb", [P, E_SLOTS, N])
        p_sb = sb("p_sb", [P, P_SLOTS, N])
        u_sb = sb("u_sb", [P, NT, N])
        r_sb = sb("r_sb", [P, NQ])
        r_rest = sb("r_rest", [P, 2, NQ])
        r_part = sb("r_part", [P, 3, NQ], BF16)
        x1 = sb("x1", [P, NT, F])
        stats = sb("stats", [P, NT, 6])
        halves = sb("halves", [P, 4, NT])
        mean = sb("mean", [P, NT])
        f_var = sb("f_var", [P, NT])
        ln_var = sb("ln_var", [P, NT])
        rstd = sb("rstd", [P, NT])
        sd_col = sb("sd_col", [P, NT, 2])
        row_max = sb("row_max", [P, NT])
        m_col = sb("m_col", [P, NT])
        u_cols = sb("u_cols", [P, 2, NT])
        d_slope = sb("d_slope", [P, NT])
        m_tmp = sb("m_tmp", [P, NT])
        den = sb("den", [P, NT])
        q_hi = u_sb[:, 0, :].bitcast(F32R)
        q_lo = u_sb[:, 1, :].bitcast(F32R)
        k_hi = u_sb[:, 2, :].bitcast(F32R)
        k_lo = u_sb[:, 3, :].bitcast(F32R)
        adj_bf = [p_sb[:, n, 0:N // 2].bitcast(BF16) for n in range(2)]
        x1T = u_sb[:, 4, :]
        wh = u_sb[:, 5, :]
        ctxT = p_sb[:, 0, :]
        y0 = p_sb[:, 1, :]
        xb = p_sb[:, 2, :]
        z0 = p_sb[:, 3, :]
        hT = e_sb[:, 0, :]
        den_sb = e_sb[:, 1, :]
        h1 = p_sb[:, 0, :]
        h_neg = p_sb[:, 1, :]
        h_exp = p_sb[:, 2, :]
        z1 = p_sb[:, 3, :]
        out_sb = p_sb[:, 7, :]

        ps = [ctx.enter_context(nc.psum_tensor(f"ps{n}", [P, N], F32)) for n in range(2)]
        ps_u = ctx.enter_context(nc.psum_tensor("ps_u", [P, N], F32))
        ps_sum = ctx.enter_context(nc.psum_tensor("ps_sum", [P, HALF], F32))
        ps_small = ctx.enter_context(nc.psum_tensor("ps_small", [P, HALF], F32))

        w_loaded = sem("w_loaded")
        adj_loaded = sem("adj_loaded")
        memsets = sem("memsets")
        consts = sem("consts")
        adj_cmp = sem("adj_cmp")
        adj_ps = sem("adj_ps")
        adj_used = sem("adj_used")
        wT_ps = sem("wT_ps")
        wT_ready = sem("wT_ready")
        wa_ps = sem("wa_ps")
        wa_ready = sem("wa_ready")
        x_loaded = sem("x_loaded")
        xT_ps = sem("xT_ps")
        xT_ready = sem("xT_ready")
        q_ps = sem("q_ps")
        k_ps = sem("k_ps")
        v_ps = sem("v_ps")
        hi_ready = sem("hi_ready")
        lo_ready = sem("lo_ready")
        v_ready = sem("v_ready")
        stacked = sem("stacked")
        scores_ready = sem("scores_ready")
        exp_ready = sem("exp_ready")
        probs_ready = sem("probs_ready")
        u_ready = sem("u_ready")
        u_saved = sem("u_saved")
        sums_done = sem("sums_done")
        r_split = sem("r_split")
        r_ps = sem("r_ps")
        u_scaled = sem("u_scaled")
        ctx_ready = sem("ctx_ready")
        o_ps = sem("o_ps")
        xb_ready = sem("xb_ready")
        var_ready = sem("var_ready")
        rstd_ready = sem("rstd_ready")
        act_chain = sem("act_chain")
        dve_chain = sem("dve_chain")
        x1_ready = sem("x1_ready")
        x1T_ps = sem("x1T_ps")
        x1T_ready = sem("x1T_ready")
        wh_ps = sem("wh_ps")
        drow_ps = sem("drow_ps")
        sd_ps = sem("sd_ps")
        sd_ready = sem("sd_ready")
        wh_ready = sem("wh_ready")
        m_ready = sem("m_ready")
        mrow_ps = sem("mrow_ps")
        slope_ready = sem("slope_ready")
        shifted = sem("shifted")
        exp1_ready = sem("exp1_ready")
        probs1_ready = sem("probs1_ready")
        h_ps = sem("h_ps")
        hT_ready = sem("hT_ready")
        den_ready = sem("den_ready")
        hp_ps = sem("hp_ps")
        neg_ready = sem("neg_ready")
        elu_exp = sem("elu_exp")
        out_ready = sem("out_ready")
        out_stored = sem("out_stored")

        DVE_CHAIN = 33

        block = ctx.enter_context(nc.Block())

        @block.sync
        def _(sp):
            sp.dma_start(u_sb[:].bitcast(I32), adj.rearrange("(t p) c -> p t c", p=P)
                         ).then_inc(adj_loaded, 16)
            for n, w in enumerate((Wq, Wk, Wv, Wo, W1)):
                sp.dma_start(w_nat[:, n, :], w).then_inc(w_loaded, 16)
            for n, b in enumerate((bq, bk)):
                sp.dma_start(bias_col[:, n:n + 1], b.rearrange("(p o) -> p o", o=1)).then_inc(w_loaded, 16)
            for n, b in enumerate((bv, bo, gamma, beta)):
                sp.dma_start(rows[:, n, :], b.rearrange("(o f) -> o f", o=1).broadcast_to([P, F])
                             ).then_inc(w_loaded, 16)
            for n in range(2):
                sp.dma_start(a_sb[:, n:n + 1], a1[n * P:(n + 1) * P, :]).then_inc(w_loaded, 16)
            sp.dma_start(x_sb[:], x[0].rearrange("(t p) f -> p t f", p=P)).then_inc(x_loaded, 16)

            def batch(i, last):
                for n, (hi, lo, st, low) in enumerate(((q_hi, q_lo, q_st, (0, 1, 0, 1)),
                                                       (k_hi, k_lo, k_st, (0, 0, 1, 1)))):
                    for part, src, done in ((0, hi, hi_ready), (1, lo, lo_ready)):
                        sp.wait_ge(done, i * 2 + n + 1)
                        for quad in range(4):
                            if low[quad] == part:
                                for h in range(HEADS):
                                    sp.dma_start(st[quad * DH:(quad + 1) * DH, h, :].bitcast(F32),
                                                 src[h * DH:(h + 1) * DH, :].bitcast(F32)
                                                 ).then_inc(stacked, 16)
                if not last:
                    sp.wait_ge(x1_ready, i + 1)
                    sp.dma_start(x_sb[:], x[bass.ds(i + 1, 1)].rearrange("a (t p) f -> p (a t) f", p=P)
                                 ).then_inc(x_loaded, 16)
                sp.wait_ge(out_ready, i + 1)
                sp.dma_start(out[bass.ds(i, 1)].rearrange("a (t p) f -> p (a t) f", p=P),
                             out_sb.rearrange("p (t f) -> p t f", f=F)).then_inc(out_stored, 16)

            with sp.Fori(0, B - 1) as i:
                batch(i, False)
            batch(B - 1, True)
            sp.wait_ge(out_stored, 16 * B)

        @block.gpsimd
        def _(pool):
            pool.memset(ident[:], 0.0).then_inc(memsets, 1)
            pool.memset(ident_bf[:], 0.0).then_inc(memsets, 1)
            pool.memset(sel[:], 0.0).then_inc(memsets, 1)
            pool.memset(quad_first[:], 0.0).then_inc(memsets, 1)
            pool.memset(one_hot[:], 0.0).then_inc(memsets, 1)
            pool.memset(ones32[:], 1.0).then_inc(consts, 1)
            pool.memset(eps_col[:], LN_EPS).then_inc(consts, 1)
            pool.wait_ge(memsets, 5)
            pool.memset(one_hot[:, DH - 1:DH], 1.0).then_inc(consts, 1)
            for m in (ident, ident_bf):
                pool.affine_select(out=m[:], in_=m[:], compare_op=ALU.not_equal, fill=1.0, base=0,
                                   pattern=[[-1, P]], channel_multiplier=1).then_inc(consts, 1)
            sel_v = sel[:].rearrange("p k (h d) -> p k h d", h=HEADS)
            pool.affine_select(out=sel_v, in_=sel_v, compare_op=ALU.not_equal, fill=1.0, base=0,
                               pattern=[[-1, NT * Q], [-DH, HEADS], [0, DH]], channel_multiplier=1
                               ).then_inc(consts, 1)
            for h in range(HEADS):
                pool.wait_ge(consts, 6 + h)
                pool.memset(quad_first[h * DH:h * DH + 1, :], 1.0).then_inc(consts, 1)
            pool.wait_ge(w_loaded, 13 * 16)

            def batch(i):
                pool.wait_ge(x_loaded, i * 16 + 16)
                pool.wait_ge(sums_done, i * NT + NT)
                pool.tensor_tensor(xb.rearrange("p (t f) -> p t f", f=F), x_sb[:],
                                   rows[:, 1:2, :].broadcast_to([P, NT, F]), ALU.add
                                   ).then_inc(xb_ready, 1)

            with pool.Fori(0, B) as i:
                batch(i)

        @block.scalar
        def _(act):
            act.preload_act_table_set("natural_log_exp_and_others")
            act.wait_ge(wT_ps, 1)
            act.activation(w_t[:, 0:4, :].rearrange("p a f -> p (a f)"), ps_u[:, 0:4 * F], ACT.Copy
                           ).then_inc(wT_ready, 1)
            act.activation(w_t[:, 4, :], ps_u[:, 4 * F:5 * F], ACT.Copy).then_inc(wT_ready, 1)

            def rstd_of(i, k):
                act.wait_ge(var_ready, i * 3 + k + 1)
                act.activation(ln_var[:], f_var[:], ACT.Ln, bias=eps_col[:], scale=1.0 / F
                               ).then_inc(act_chain, 1)
                act.wait_ge(act_chain, i * 3 + k + 1)
                act.activation(rstd[:], ln_var[:], ACT.Exp, scale=-0.5).then_inc(rstd_ready, 1)

            def batch(i):
                act.wait_ge(xT_ps, i + 1)
                act.activation(xT[:], ps[0][:], ACT.Copy).then_inc(xT_ready, 1)
                act.wait_ge(q_ps, i + 1)
                act.activation(q_hi, ps[1][:], ACT.Identity, bias=bias_col[:, 0:1]).then_inc(hi_ready, 1)
                act.wait_ge(k_ps, i + 1)
                act.activation(k_hi, ps[0][:], ACT.Identity, bias=bias_col[:, 1:2]).then_inc(hi_ready, 1)

                def save_u(j, half):
                    act.wait_ge(u_ready, i * NT * NH + j * NH + half + 1)
                    if j < 4 and half == 0:
                        act.wait_ge(stacked, i * STACKS * 16 + STACKS * 16)
                    act.activation(u_sb[:, j, half * HALF:(half + 1) * HALF],
                                   ps_u[:, half * HALF:(half + 1) * HALF], ACT.Copy).then_inc(u_saved, 1)

                for j in range(NT):
                    for h in range(HEADS):
                        g = j * HEADS + h
                        act.wait_ge(scores_ready, i * NT * HEADS + g + 1)
                        if g >= E_SLOTS:
                            act.wait_ge(probs_ready, i * NT * HEADS + g - E_SLOTS + 1)
                        act.activation(e_sb[:, g % E_SLOTS, :], ps[g % 2][:], ACT.Exp, scale=SCALE
                                       ).then_inc(exp_ready, 1)
                        if j and h in (1, 2):
                            save_u(j - 1, h - 1)
                save_u(NT - 1, 0)
                save_u(NT - 1, 1)
                rstd_of(i, 0)
                rstd_of(i, 1)
                act.wait_ge(x1T_ps, i + 1)
                act.activation(x1T, ps[0][:], ACT.Copy).then_inc(x1T_ready, 1)
                act.wait_ge(wh_ps, i + 1)
                act.activation(wh, ps[1][:], ACT.Copy).then_inc(wh_ready, 1)
                act.wait_ge(mrow_ps, i * 2 + 1)

                def exp1(t):
                    act.wait_ge(shifted, i * NT + t + 1)
                    act.activation(e_sb[:, t % E_SLOTS, :], e_sb[:, t % E_SLOTS, :], ACT.Exp
                                   ).then_inc(exp1_ready, 1)

                for t in range(NT):
                    if t >= E_SLOTS:
                        act.wait_ge(probs1_ready, i * NT + t - E_SLOTS + 1)
                    act.activation(e_sb[:, t % E_SLOTS, :], ps[0][:], ACT.Identity,
                                   bias=d_slope[:, t:t + 1]).then_inc(slope_ready, 1)
                    if t:
                        exp1(t - 1)
                exp1(NT - 1)
                act.wait_ge(h_ps, i + 1)
                act.wait_ge(probs1_ready, i * NT + NT)
                act.activation(hT, ps_u[:], ACT.Copy).then_inc(hT_ready, 1)
                act.wait_ge(neg_ready, i + 1)
                act.activation(h_exp, h_neg, ACT.Exp).then_inc(elu_exp, 1)
                rstd_of(i, 2)

            with act.Fori(0, B) as i:
                batch(i)

        @block.tensor
        def _(pe):
            pe.wait_ge(consts, 10)
            pe.wait_ge(w_loaded, 13 * 16)
            for n in range(5):
                mm = pe.transpose(ps_u[:, n * F:(n + 1) * F], w_nat[:, n, :], ident[:])
            mm.then_inc(wT_ps, 1)
            for t in range(NT):
                pe.wait_ge(adj_cmp, 3 * t + 2)
                if t:
                    pe.wait_ge(adj_used, 2 * t)
                for m in range(2):
                    dst = ps[m][:].bitcast(BF16)
                    for c in range(NT):
                        mm = pe.transpose(dst[:, c * P:(c + 1) * P], adj_bf[m][:, c * P:(c + 1) * P],
                                          ident_bf[:])
                    mm.then_inc(adj_ps, 1)
            pe.wait_ge(wT_ready, 2)
            pe.matmul(ps_small[:, 0:2], w_t[:, 4, :], a_sb[:], start=True, stop=True).then_inc(wa_ps, 1)
            pe.wait_ge(wa_ready, 1)
            pe.wait_ge(adj_used, 2 * NT)

            def batch(i):
                pe.wait_ge(x_loaded, i * 16 + 16)
                for t in range(NT):
                    mm = pe.transpose(ps[0][:, t * P:(t + 1) * P], x_sb[:, t, :], ident[:])
                mm.then_inc(xT_ps, 1)
                pe.wait_ge(xT_ready, i + 1)
                for n, (dst, done) in enumerate(((ps[1], q_ps), (ps[0], k_ps))):
                    for half in range(NH):
                        s = slice(half * HALF, (half + 1) * HALF)
                        mm = pe.matmul(dst[:, s], w_t[:, n, :], xT[:, s], start=True, stop=True)
                    mm.then_inc(done, 1)
                for t in range(NT):
                    mm = pe.matmul(ps_u[:, t * P:(t + 1) * P], xT[:, t * P:(t + 1) * P], w_t[:, 2, :],
                                   start=True, stop=True)
                mm.then_inc(v_ps, 1)

                def scores(j, h):
                    g = j * HEADS + h
                    if g < 2:
                        pe.wait_ge(lo_ready, i * 2 + 2)
                        pe.wait_ge(stacked, i * STACKS * 16 + STACKS * 16)
                    else:
                        pe.wait_ge(exp_ready, i * NT * HEADS + g - 1)
                    for half in range(NH):
                        s = slice(half * HALF, (half + 1) * HALF)
                        mm = pe.matmul(ps[g % 2][:, s], k_st[:, h, j * P:(j + 1) * P], q_st[:, h, s],
                                       start=True, stop=True)
                    mm.then_inc(scores_ready, 1)

                def probs(j, h):
                    return p_sb[:, (j * HEADS + h) % P_SLOTS, :]

                def times_v(j, half):
                    if half == 0:
                        pe.wait_ge(probs_ready, i * NT * HEADS + (j + 1) * HEADS)
                    if j:
                        pe.wait_ge(u_saved, i * NT * NH + (j - 1) * NH + half + 1)
                    else:
                        pe.wait_ge(v_ready, i + 1)
                    s = slice(half * HALF, (half + 1) * HALF)
                    for h in range(HEADS):
                        d = slice(h * DH, (h + 1) * DH)
                        mm = pe.matmul(ps_u[d, s], v_sb[:, j, d], probs(j, h)[:, s], start=True, stop=True)
                    mm.then_inc(u_ready, 1)

                def sums(j, quarters):
                    for c in quarters:
                        k = j * Q + c
                        for h in range(HEADS):
                            mm = pe.matmul(ps_sum[h * DH:(h + 1) * DH, 0:NQ],
                                           one_hot[:, DH - 1 - k:2 * DH - 1 - k],
                                           probs(j, h)[:, c * NQ:(c + 1) * NQ],
                                           start=(k == 0), stop=(k == NT * Q - 1),
                                           skip_group_check=True)
                    if c == Q - 1:
                        mm.then_inc(sums_done, 1)

                for j in range(NT + 1):
                    for h in range(HEADS):
                        if j < NT:
                            scores(j, h)
                        if j:
                            (lambda: times_v(j - 1, 0), lambda: times_v(j - 1, 1),
                             lambda: sums(j - 1, (0, 1)), lambda: sums(j - 1, (2, 3)))[h]()

                pe.wait_ge(r_split, i + 1)
                pe.wait_ge(exp_ready, (i + 1) * NT * HEADS)
                for j in range(NT):
                    if j >= 2:
                        pe.wait_ge(u_scaled, i * NT + j - 1)
                    for c in range(Q):
                        for n in range(3):
                            mm = pe.matmul(ps[j % 2][:, c * NQ:(c + 1) * NQ], sel[:, j * Q + c, :],
                                           r_part[:, n, :], start=(n == 0), stop=(n == 2))
                    mm.then_inc(r_ps, 1)
                pe.wait_ge(ctx_ready, i + 1)
                pe.wait_ge(u_saved, (i + 1) * NT * NH)
                for t in range(NT):
                    mm = pe.matmul(ps_u[:, t * P:(t + 1) * P], ctxT[:, t * P:(t + 1) * P], w_t[:, 3, :],
                                   start=True, stop=True)
                mm.then_inc(o_ps, 1)

                pe.wait_ge(x1_ready, i + 1)
                for t in range(NT):
                    mm = pe.transpose(ps[0][:, t * P:(t + 1) * P], x1[:, t, :], ident[:])
                mm.then_inc(x1T_ps, 1)
                pe.wait_ge(x1T_ready, i + 1)
                for half in range(NH):
                    s = slice(half * HALF, (half + 1) * HALF)
                    mm = pe.matmul(ps[0][:, s], wa[:, 1:2].broadcast_to([P, P]), x1T[:, s],
                                   start=True, stop=True)
                mm.then_inc(drow_ps, 1)
                for t in range(NT):
                    mm = pe.matmul(ps_small[:, 2 * t:2 * t + 2], x1T[:, t * P:(t + 1) * P], wa[:],
                                   start=True, stop=True)
                mm.then_inc(sd_ps, 1)
                for t in range(NT):
                    mm = pe.matmul(ps[1][:, t * P:(t + 1) * P], x1T[:, t * P:(t + 1) * P], w_nat[:, 4, :],
                                   start=True, stop=True)
                mm.then_inc(wh_ps, 1)
                pe.wait_ge(m_ready, i + 1)
                pe.wait_ge(wh_ready, i + 1)
                for n, dst in ((1, ps[0]), (0, ps[1])):
                    for t in range(NT):
                        mm = pe.matmul(dst[:, t * P:(t + 1) * P],
                                       u_cols[:, n, t:t + 1].broadcast_to([P, P]),
                                       ident[:], start=True, stop=True)
                    mm.then_inc(mrow_ps, 1)
                for t in range(NT):
                    pe.wait_ge(probs1_ready, i * NT + t + 1)
                    for half in range(NH):
                        s = slice(half * HALF, (half + 1) * HALF)
                        pe.matmul(ps_u[:, s], wh[:, t * P:(t + 1) * P], p_sb[:, t, s],
                                  start=(t == 0), stop=(t == NT - 1), skip_group_check=True)
                    if t % 4 == 3:
                        for half in range(NH):
                            s = slice(half * HALF, (half + 1) * HALF)
                            for c in range(4):
                                mm = pe.matmul((ps_sum, ps_small)[half][c * DH:(c + 1) * DH, :], ones32[:],
                                               p_sb[:, t - 3 + c, s], start=(t == 3),
                                               stop=(t == NT - 1), skip_group_check=True)
                mm.then_inc(h_ps, 1)
                pe.wait_ge(hT_ready, i + 1)
                pe.wait_ge(den_ready, i * 2 + 2)
                for t in range(NT):
                    pe.matmul(ps[0][:, t:t + 1], den_sb[:, t * P:(t + 1) * P], quad_first[:],
                              start=True, stop=True)
                for t in range(NT):
                    mm = pe.transpose(ps[1][:, t * P:(t + 1) * P], hT[:, t * P:(t + 1) * P], ident[:])
                mm.then_inc(hp_ps, 1)
                pe.wait_ge(out_ready, i + 1)

            with pe.Fori(0, B) as i:
                batch(i)

        @block.vector
        def _(dve):
            dve.wait_ge(consts, 10)
            dve.wait_ge(adj_loaded, 16)
            for t in range(NT):
                a_t = u_sb[:, t, :].bitcast(I32)
                if t:
                    dve.wait_ge(adj_ps, 2 * t)
                    dve.wait_ge(adj_cmp, 3 * t)
                dve.tensor_scalar(adj_bf[0], a_t, 0.0, None, ALU.not_equal).then_inc(adj_cmp, 1)
                dve.tensor_scalar(adj_bf[1], a_t, 0.0, None, ALU.is_gt).then_inc(adj_cmp, 1)
                dve.wait_ge(adj_cmp, 3 * t + 2)
                dve.tensor_scalar(bias_n[:, t, :], adj_bf[1], -1.0, -NEG_BIG, ALU.add, ALU.mult
                                  ).then_inc(adj_cmp, 1)
                dve.wait_ge(adj_ps, 2 * (t + 1))
                q = slice(t * P, (t + 1) * P)
                for m, dst, a, b, op1 in ((0, clip_t, HI, LO, ALU.max), (1, keep_t, 255.0, 0.0, ALU.add)):
                    dve.tensor_scalar(dst[:, :, q],
                                      ps[m][:].bitcast(BF16)[:, 0:N].rearrange("p (c q) -> p c q", q=P),
                                      a, b, ALU.mult, op1).then_inc(adj_used, 1)
            dve.wait_ge(wa_ps, 1)
            dve.tensor_copy(wa[:], ps_small[:, 0:2]).then_inc(wa_ready, 1)

            def batch(i):
                steps = [0]

                def chain(ins):
                    steps[0] += 1
                    ins.then_inc(dve_chain, 1)
                    dve.wait_ge(dve_chain, i * DVE_CHAIN + steps[0])

                def tiles(ap):
                    return ap.rearrange("p (t f) -> p t f", f=F)

                def layernorm(src, dst, k, done):
                    for t in range(NT):
                        ins = dve.bn_stats(stats[:, t, :], src[:, t, :])
                    chain(ins)
                    dve.tensor_tensor(halves[:, 0, :], stats[:, :, 1], stats[:, :, 4], ALU.add)
                    dve.tensor_tensor(halves[:, 2, :], stats[:, :, 2], stats[:, :, 5], ALU.add)
                    chain(dve.tensor_tensor(halves[:, 1, :], stats[:, :, 1], stats[:, :, 4], ALU.subtract))
                    dve.tensor_scalar(mean[:], halves[:, 0, :], 0.5, None, ALU.mult)
                    chain(dve.tensor_tensor(halves[:, 3, :], halves[:, 1, :], halves[:, 1, :], ALU.mult))
                    dve.scalar_tensor_tensor(out=f_var[:], in0=halves[:, 3, :], scalar=F / 4,
                                             in1=halves[:, 2, :], op0=ALU.mult, op1=ALU.add
                                             ).then_inc(var_ready, 1)
                    dve.wait_ge(rstd_ready, i * 3 + k + 1)
                    for t in range(NT):
                        ins = dve.tensor_scalar(dst[:, t, :], src[:, t, :], mean[:, t:t + 1],
                                                rstd[:, t:t + 1], ALU.subtract, ALU.mult)
                    done(ins)

                for n, (src, hi, lo, ready) in enumerate(((ps[1], q_hi, q_lo, None),
                                                          (ps[0], k_hi, k_lo, None))):
                    dve.wait_ge(hi_ready, i * 2 + n + 1)
                    dve.scalar_tensor_tensor(out=lo, in0=src[:], scalar=bias_col[:, n:n + 1],
                                             in1=hi.bitcast(F32), op0=ALU.add, op1=ALU.subtract
                                             ).then_inc(lo_ready, 1)
                dve.wait_ge(v_ps, i + 1)
                dve.tensor_tensor(v_sb[:], tiles(ps_u[:]), rows[:, 0:1, :].broadcast_to([P, NT, F]),
                                  ALU.add).then_inc(v_ready, 1)

                for j in range(NT):
                    if j >= 2:
                        dve.wait_ge(sums_done, i * NT + j - 1)
                    for h in range(HEADS):
                        g = j * HEADS + h
                        dve.wait_ge(exp_ready, i * NT * HEADS + g + 1)
                        dve.scalar_tensor_tensor(out=p_sb[:, g % P_SLOTS, :], in0=e_sb[:, g % E_SLOTS, :],
                                                 scalar=LO, in1=clip_t[:, j, :], op0=ALU.max,
                                                 op1=ALU.min).then_inc(probs_ready, 1)

                dve.wait_ge(sums_done, i * NT + NT)
                chain(dve.reciprocal(r_sb[:], ps_sum[:, 0:NQ]))
                chain(dve.tensor_copy(r_part[:, 0, :], r_sb[:]))
                chain(dve.tensor_tensor(r_rest[:, 0, :], r_sb[:], r_part[:, 0, :], ALU.subtract))
                chain(dve.tensor_copy(r_part[:, 1, :], r_rest[:, 0, :]))
                chain(dve.tensor_tensor(r_rest[:, 1, :], r_rest[:, 0, :], r_part[:, 1, :], ALU.subtract))
                dve.tensor_copy(r_part[:, 2, :], r_rest[:, 1, :]).then_inc(r_split, 1)
                dve.wait_ge(u_saved, (i + 1) * NT * NH)
                for j in range(NT):
                    dve.wait_ge(r_ps, i * NT + j + 1)
                    dst = ctxT if j == 0 else u_sb[:, j, :]
                    dve.tensor_tensor(dst, u_sb[:, j, :], ps[j % 2][:], ALU.mult).then_inc(u_scaled, 1)
                    if j:
                        dve.wait_ge(u_scaled, i * NT + j + 1)
                        ins = dve.tensor_tensor(ctxT, ctxT, u_sb[:, j, :], ALU.add)
                        if j < NT - 1:
                            chain(ins)
                ins.then_inc(ctx_ready, 1)
                dve.wait_ge(o_ps, i + 1)
                dve.wait_ge(xb_ready, i + 1)
                chain(dve.tensor_tensor(y0, ps_u[:], xb, ALU.add))
                layernorm(tiles(y0), tiles(z0), 0, chain)
                chain(dve.tensor_tensor(tiles(y0), tiles(z0), rows[:, 2:3, :].broadcast_to([P, NT, F]),
                                        ALU.mult))
                chain(dve.tensor_tensor(tiles(z0), tiles(y0), rows[:, 3:4, :].broadcast_to([P, NT, F]),
                                        ALU.add))
                chain(dve.tensor_tensor(tiles(y0), tiles(z0), x_sb[:], ALU.add))
                layernorm(tiles(y0), x1, 1, lambda ins: ins.then_inc(x1_ready, 1))

                dve.wait_ge(drow_ps, i + 1)
                dve.wait_ge(sd_ps, i + 1)
                dve.tensor_copy(sd_col[:].rearrange("p t c -> p (t c)"), ps_small[:, 0:2 * NT]
                                ).then_inc(sd_ready, 1)
                for t in range(NT):
                    ins = dve.tensor_tensor_reduce(p_sb[:, t, :], ps[0][:], bias_n[:, t, :], 1.0, NEG_BIG,
                                                   ALU.add, ALU.max, row_max[:, t:t + 1])
                chain(ins)
                dve.wait_ge(sd_ready, i + 1)
                chain(dve.tensor_tensor(m_tmp[:], row_max[:], sd_col[:, :, 0], ALU.add))
                dve.tensor_scalar(d_slope[:], sd_col[:, :, 1], NEG_SLOPE, None, ALU.mult)
                chain(dve.scalar_tensor_tensor(out=m_col[:], in0=m_tmp[:], scalar=NEG_SLOPE, in1=m_tmp[:],
                                               op0=ALU.mult, op1=ALU.max))
                dve.tensor_tensor(u_cols[:, 0, :], sd_col[:, :, 0], m_col[:], ALU.subtract)
                dve.scalar_tensor_tensor(out=u_cols[:, 1, :], in0=sd_col[:, :, 0], scalar=NEG_SLOPE,
                                         in1=m_col[:], op0=ALU.mult, op1=ALU.subtract).then_inc(m_ready, 1)
                dve.wait_ge(mrow_ps, i * 2 + 2)

                def mask1(t):
                    dve.wait_ge(exp1_ready, i * NT + t + 1)
                    dve.tensor_tensor(p_sb[:, t, :], e_sb[:, t % E_SLOTS, :], keep_t[:, t, :], ALU.min
                                      ).then_inc(probs1_ready, 1)

                for t in range(NT):
                    dve.wait_ge(slope_ready, i * NT + t + 1)
                    dve.scalar_tensor_tensor(out=e_sb[:, t % E_SLOTS, :], in0=ps[1][:],
                                             scalar=sd_col[:, t, 1:2], in1=e_sb[:, t % E_SLOTS, :],
                                             op0=ALU.add, op1=ALU.max).then_inc(shifted, 1)
                    if t:
                        mask1(t - 1)
                mask1(NT - 1)
                dve.wait_ge(h_ps, i + 1)
                dve.tensor_copy(den_sb[:, 0:HALF], ps_sum[:]).then_inc(den_ready, 1)
                dve.tensor_copy(den_sb[:, HALF:N], ps_small[:]).then_inc(den_ready, 1)
                dve.wait_ge(hp_ps, i + 1)
                chain(dve.reciprocal(den[:], ps[0][:, 0:NT]))
                chain(dve.tensor_tensor(tiles(h1), tiles(ps[1][:]),
                                        den[:].unsqueeze(2).broadcast_to([P, NT, F]), ALU.mult))
                dve.tensor_scalar(h_neg, h1, 0.0, None, ALU.min).then_inc(neg_ready, 1)
                chain(dve.tensor_scalar(z1, h1, 0.0, -1.0, ALU.max, ALU.add))
                chain(dve.tensor_tensor(tiles(z1), tiles(z1), x1[:], ALU.add))
                dve.wait_ge(elu_exp, i + 1)
                chain(dve.tensor_tensor(h1, z1, h_exp, ALU.add))
                layernorm(tiles(h1), tiles(out_sb), 2, lambda ins: ins.then_inc(out_ready, 1))
                dve.wait_ge(out_stored, i * 16 + 16)
                assert steps[0] == DVE_CHAIN, steps

            with dve.Fori(0, B) as i:
                batch(i)


_INS = ["x", "adj", "L0_gnn_Wq", "L0_gnn_bq", "L0_gnn_Wk", "L0_gnn_bk", "L0_gnn_Wv", "L0_gnn_bv",
        "L0_gnn_Wo", "L0_gnn_bo", "L0_gnn_gamma", "L0_gnn_beta", "L1_gnn_W", "L1_gnn_a"]


def kernel(**inputs):
    import numpy as _np
    import concourse.bacc as _bacc
    from concourse import mybir as _mybir
    from concourse.bass_utils import run_bass_kernel_spmd as _run

    nc = _bacc.Bacc("TRN2", target_bir_lowering=False, num_devices=1)
    arrays, args = {}, []
    for name in _INS:
        a = _np.ascontiguousarray(inputs[name])
        arrays[f"in_{name}"] = a
        args.append(nc.dram_tensor(f"in_{name}", a.shape, _mybir.dt.from_np(a.dtype),
                                   kind="ExternalInput").ap())
    shape = tuple(inputs["x"].shape)
    args.append(nc.dram_tensor("out_dram", shape, _mybir.dt.from_np(_np.dtype("float32")),
                               kind="ExternalOutput").ap())
    build(nc, *args)
    r = _run(nc, [arrays], core_ids=[0])
    return r.results[0]["out_dram"]
```

```python
import math
from contextlib import ExitStack

import numpy as np

import concourse.bass as bass
from concourse import mybir

F32 = mybir.dt.float32
F32R = mybir.dt.float32r
BF16 = mybir.dt.bfloat16
U8 = mybir.dt.uint8
I32 = mybir.dt.int32
ALU = mybir.AluOpType
ACT = mybir.ActivationFunctionType
AX = mybir.AxisListType

P = 128
HEADS = 4
SCORE_CLIP = 10.0
NEG_SLOPE = 0.2
LN_EPS = 1e-5
NEG_BIG = -1e30


def build(nc, x, adj, Wq, bq, Wk, bk, Wv, bv, Wo, bo, gamma, beta, W1, a1, out):
    B, N, F = x.shape
    assert F == P and N % P == 0
    NT = N // P
    DH = F // HEADS
    HALF = 512
    NH = N // HALF
    Q = 4
    NQ = N // Q
    assert NT * Q == DH and NT == 8
    SCALE = 1.0 / math.sqrt(DH)
    LO = float(np.exp(np.float32(-SCORE_CLIP)))
    HI = float(np.exp(np.float32(SCORE_CLIP)))
    E_SLOTS = 3
    LAG = 2
    P_SLOTS = 2 * HEADS
    SEL_ROWS = NT * Q * P // N
    EARLY = 4
    STACKS = 8 * HEADS
    GROUPS = ((0, 1), (2, 3), (4, 5), (6, 7))
    last_of = {g[-1]: n for n, g in enumerate(GROUPS)}

    with ExitStack() as ctx:
        def sb(name, shape, dt=F32):
            return ctx.enter_context(nc.sbuf_tensor(name, shape, dt))

        def sem(name):
            return ctx.enter_context(nc.semaphore(name))

        ident = sb("ident", [P, P])
        ident_bf = sb("ident_bf", [P, P], BF16)
        ones32 = sb("ones32", [P, DH])
        one_hot = sb("one_hot", [P, 2 * DH - 1])
        sel = sb("sel", [P, NT * Q, P], F32R)
        quad_first = sb("quad_first", [P, 1])
        w_nat = sb("w_nat", [P, 5, F])
        w_t = sb("w_t", [P, 5, F])
        bias_col = sb("bias_col", [P, 2])
        rows = sb("rows", [P, 4, F])
        a_sb = sb("a_sb", [P, 2])
        wa = sb("wa", [P, 2])
        eps_col = sb("eps_col", [P, 1])
        clip_t = sb("clip_t", [P, NT, N])
        keep_t = sb("keep_t", [P, NT, N], U8)
        bias_n = sb("bias_n", [P, NT, N], BF16)
        x_sb = sb("x_sb", [P, NT, F])
        xT = sb("xT", [P, N])
        k_st = sb("k_st", [P, HEADS, N], F32R)
        q_st = sb("q_st", [P, HEADS, N], F32R)
        v_sb = sb("v_sb", [P, NT, F])
        e_sb = sb("e_sb", [P, E_SLOTS, N])
        p_sb = sb("p_sb", [P, P_SLOTS, N])
        u_sb = sb("u_sb", [P, NT, N])
        r_part = sb("r_part", [P, 2, NQ], F32R)
        x1 = sb("x1", [P, NT, F])
        stats = sb("stats", [P, NT, 6])
        halves = sb("halves", [P, 4, NT])
        mean = sb("mean", [P, NT])
        f_var = sb("f_var", [P, NT])
        ln_var = sb("ln_var", [P, NT])
        rstd_col = sb("rstd_col", [P, NT])
        sd_col = sb("sd_col", [P, NT, 2])
        row_max = sb("row_max", [P, NT])
        m_col = sb("m_col", [P, NT])
        u_cols = sb("u_cols", [P, 2, NT])
        d_slope = sb("d_slope", [P, NT])
        m_tmp = sb("m_tmp", [P, NT])
        den = sb("den", [P, NT])
        q_hi = u_sb[:, 0, :].bitcast(F32R)
        q_lo = u_sb[:, 1, :].bitcast(F32R)
        k_hi = u_sb[:, 2, :].bitcast(F32R)
        k_lo = u_sb[:, 3, :].bitcast(F32R)
        adj_bf = [p_sb[:, n, 0:N // 2].bitcast(BF16) for n in range(2)]
        x1T = u_sb[:, 4, :]
        wh = u_sb[:, 5, :]
        r_sb = e_sb[:, 0, 0:NQ]
        parts = [p_sb[:, n, :] for n in (0, 6, 7, 0)]
        y0 = p_sb[:, 1, :]
        xb = p_sb[:, 2, :]
        z0 = p_sb[:, 3, :]
        x_beta = p_sb[:, 4, :]
        g0 = p_sb[:, 5, :]
        hT = u_sb[:, 4, :]
        h_exp = u_sb[:, 5, :]
        h1 = u_sb[:, 6, :]
        den_sb = u_sb[:, 7, :]
        z1 = u_sb[:, 7, :]
        out_sb = u_sb[:, 7, :]

        ps = [ctx.enter_context(nc.psum_tensor(f"ps{n}", [P, N], F32)) for n in range(2)]
        ps_u = ctx.enter_context(nc.psum_tensor("ps_u", [P, N], F32))
        ps_rest = ctx.enter_context(nc.psum_tensor("ps_rest", [P, N], F32))
        ps_sum = ps_rest[:, 0:HALF]
        ps_small = ps_rest[:, HALF:N]

        w_loaded = sem("w_loaded")
        adj_loaded = sem("adj_loaded")
        memsets = sem("memsets")
        consts = sem("consts")
        sel_ready = sem("sel_ready")
        adj_cmp = sem("adj_cmp")
        adj_ps = sem("adj_ps")
        adj_used = sem("adj_used")
        wT_ps = sem("wT_ps")
        wT_ready = sem("wT_ready")
        wa_ps = sem("wa_ps")
        wa_ready = sem("wa_ready")
        x_loaded = sem("x_loaded")
        xT_ps = sem("xT_ps")
        xT_ready = sem("xT_ready")
        q_ps = sem("q_ps")
        k_ps = sem("k_ps")
        v_ps = sem("v_ps")
        hi_ready = sem("hi_ready")
        lo_ready = sem("lo_ready")
        v_ready = sem("v_ready")
        stacked = sem("stacked")
        scores_ready = sem("scores_ready")
        exp_ready = sem("exp_ready")
        probs_ready = sem("probs_ready")
        u_ready = sem("u_ready")
        u_saved = sem("u_saved")
        sums_done = sem("sums_done")
        r_split = sem("r_split")
        r_ps = sem("r_ps")
        u_scaled = sem("u_scaled")
        projected = sem("projected")
        added = sem("added")
        o_ps = sem("o_ps")
        xb_ready = sem("xb_ready")
        var_ready = sem("var_ready")
        rstd_ready = sem("rstd_ready")
        act_chain = sem("act_chain")
        dve_chain = sem("dve_chain")
        x1_ready = sem("x1_ready")
        x1T_ps = sem("x1T_ps")
        x1T_ready = sem("x1T_ready")
        wh_ps = sem("wh_ps")
        drow_ps = sem("drow_ps")
        sd_ps = sem("sd_ps")
        sd_ready = sem("sd_ready")
        wh_ready = sem("wh_ready")
        m_ready = sem("m_ready")
        mrow_ps = sem("mrow_ps")
        slope_ready = sem("slope_ready")
        shifted = sem("shifted")
        exp1_ready = sem("exp1_ready")
        probs1_ready = sem("probs1_ready")
        h_ps = sem("h_ps")
        hT_ready = sem("hT_ready")
        den_ready = sem("den_ready")
        hp_ps = sem("hp_ps")
        den_inv = sem("den_inv")
        h1_ready = sem("h1_ready")
        elu_exp = sem("elu_exp")
        out_ready = sem("out_ready")
        out_stored = sem("out_stored")

        ADDS = sum(len(g) - 1 for g in GROUPS) + 1
        DVE_CHAIN = 24
        ACT_CHAIN = 4

        def adds_before(j):
            return sum(1 for g in GROUPS for c in g[1:] if c < j)

        TAIL_PE = {5: "turn"}
        TAIL_ACT = {3: "save", 5: "divide", 7: "elu", 17: "rstd"}
        TAIL_DVE = {3: "den", 4: "inverse", 7: "residual", 9: "elu", 11: "stats0", 13: "stats1",
                    15: "variance", 19: "out0", 21: "out1"}

        block = ctx.enter_context(nc.Block())

        @block.sync
        def _(sp):
            sp.dma_start(u_sb[:].bitcast(I32), adj.rearrange("(t p) c -> p t c", p=P)
                         ).then_inc(adj_loaded, 16)
            for n, w in enumerate((Wq, Wk, Wv, Wo, W1)):
                sp.dma_start(w_nat[:, n, :], w).then_inc(w_loaded, 16)
            for n, b in enumerate((bq, bk)):
                sp.dma_start(bias_col[:, n:n + 1], b.rearrange("(p o) -> p o", o=1)).then_inc(w_loaded, 16)
            for n, b in enumerate((bv, bo, gamma, beta)):
                sp.dma_start(rows[:, n, :], b.rearrange("(o f) -> o f", o=1).broadcast_to([P, F])
                             ).then_inc(w_loaded, 16)
            sp.dma_start(a_sb[:, 0:1], a1[0:P, :]).then_inc(w_loaded, 16)
            sp.dma_start(a_sb[:, 1:2], a1[P:2 * P, :]).then_inc(out_stored, 16)
            sp.dma_start(x_sb[:], x[0].rearrange("(t p) f -> p t f", p=P)).then_inc(x_loaded, 16)

            def stack(i):
                for n, (hi, lo, st, low) in enumerate(((q_hi, q_lo, q_st, (0, 1, 0, 1)),
                                                       (k_hi, k_lo, k_st, (0, 0, 1, 1)))):
                    for part, src, done in ((0, hi, hi_ready), (1, lo, lo_ready)):
                        sp.wait_ge(done, i * 2 + n + 1)
                        for quad in range(4):
                            if low[quad] == part:
                                for h in range(HEADS):
                                    sp.dma_start(st[quad * DH:(quad + 1) * DH, h, :].bitcast(F32),
                                                 src[h * DH:(h + 1) * DH, :].bitcast(F32)
                                                 ).then_inc(stacked, 16)

            def batch(i, last):
                if not last:
                    sp.wait_ge(xb_ready, i * 2 + 2)
                    sp.dma_start(x_sb[:], x[bass.ds(i + 1, 1)].rearrange("a (t p) f -> p (a t) f", p=P)
                                 ).then_inc(x_loaded, 16)
                    stack(i + 1)
                sp.wait_ge(out_ready, i + 1)
                sp.dma_start(out[bass.ds(i, 1)].rearrange("a (t p) f -> p (a t) f", p=P),
                             out_sb.rearrange("p (t f) -> p t f", f=F)).then_inc(out_stored, 16)

            stack(0)
            with sp.Fori(0, B - 1) as i:
                batch(i, False)
            batch(B - 1, True)
            sp.wait_ge(out_stored, 16 * B + 16)

        @block.gpsimd
        def _(pool):
            pool.memset(ident[:], 0.0).then_inc(memsets, 1)
            pool.memset(ident_bf[:], 0.0).then_inc(memsets, 1)
            pool.memset(p_sb[:, 2:2 + SEL_ROWS, :], 0.0).then_inc(memsets, 1)
            pool.memset(quad_first[:], 0.0).then_inc(memsets, 1)
            pool.memset(one_hot[:], 0.0).then_inc(memsets, 1)
            pool.memset(ones32[:], 1.0).then_inc(consts, 1)
            pool.memset(eps_col[:], LN_EPS).then_inc(consts, 1)
            pool.wait_ge(memsets, 5)
            pool.memset(one_hot[:, DH - 1:DH], 1.0).then_inc(consts, 1)
            for m in (ident, ident_bf):
                pool.affine_select(out=m[:], in_=m[:], compare_op=ALU.not_equal, fill=1.0, base=0,
                                   pattern=[[-1, P]], channel_multiplier=1).then_inc(consts, 1)
            sel_v = p_sb[:, 2:2 + SEL_ROWS, :].rearrange("p a (k h d) -> p (a k) h d", h=HEADS, d=DH)
            pool.affine_select(out=sel_v, in_=sel_v, compare_op=ALU.not_equal, fill=1.0, base=0,
                               pattern=[[-1, NT * Q], [-DH, HEADS], [0, DH]], channel_multiplier=1
                               ).then_inc(consts, 1)
            for h in range(HEADS):
                pool.wait_ge(consts, 6 + h)
                pool.memset(quad_first[h * DH:h * DH + 1, :], 1.0).then_inc(consts, 1)
            pool.wait_ge(w_loaded, 12 * 16)

            def batch(i):
                pool.wait_ge(x_loaded, i * 16 + 16)
                pool.wait_ge(u_ready, (i + 1) * NT * NH)
                for dst, row in ((xb, 1), (x_beta, 3)):
                    pool.tensor_tensor(dst.rearrange("p (t f) -> p t f", f=F), x_sb[:],
                                       rows[:, row:row + 1, :].broadcast_to([P, NT, F]), ALU.add
                                       ).then_inc(xb_ready, 1)

            with pool.Fori(0, B) as i:
                batch(i)

        @block.scalar
        def _(act):
            act.preload_act_table_set("natural_log_exp_and_others")
            act.wait_ge(consts, 10)
            act.activation(sel[:].rearrange("p k m -> p (k m)"),
                           p_sb[:, 2:2 + SEL_ROWS, :].rearrange("p a c -> p (a c)"), ACT.Copy
                           ).then_inc(sel_ready, 1)
            act.wait_ge(wT_ps, 1)
            act.activation(w_t[:, 0:4, :].rearrange("p a f -> p (a f)"), ps_u[:, 0:4 * F], ACT.Copy
                           ).then_inc(wT_ready, 1)
            act.activation(w_t[:, 4, :], ps_u[:, 4 * F:5 * F], ACT.Copy).then_inc(wT_ready, 1)

            def rstd_of(i, k, step):
                act.wait_ge(var_ready, i * 3 + k + 1)
                act.activation(ln_var[:], f_var[:], ACT.Ln, bias=eps_col[:], scale=1.0 / F
                               ).then_inc(act_chain, 1)
                act.wait_ge(act_chain, i * ACT_CHAIN + step)
                act.activation(rstd_col[:], ln_var[:], ACT.Exp, scale=-0.5).then_inc(rstd_ready, 1)

            def save_xT(i):
                act.wait_ge(xT_ps, i + 1)
                act.activation(xT[:], ps[0][:], ACT.Copy).then_inc(xT_ready, 1)

            def high_parts(i):
                act.wait_ge(q_ps, i + 1)
                act.activation(q_hi, ps[1][:], ACT.Identity, bias=bias_col[:, 0:1]).then_inc(hi_ready, 1)
                act.wait_ge(k_ps, i + 1)
                act.activation(k_hi, ps[0][:], ACT.Identity, bias=bias_col[:, 1:2]).then_inc(hi_ready, 1)

            def first_layer(i, tail):
                def save_u(j, half):
                    act.wait_ge(u_ready, i * NT * NH + j * NH + half + 1)
                    if half == 0:
                        if j == 0:
                            act.wait_ge(stacked, i * STACKS * 16 + STACKS * 16)
                        elif j == 5 and tail:
                            act.wait_ge(out_ready, i)
                        elif j == NT - 1:
                            act.wait_ge(out_stored, i * 16 + 16)
                    act.activation(u_sb[:, j, half * HALF:(half + 1) * HALF],
                                   ps_u[:, half * HALF:(half + 1) * HALF], ACT.Copy).then_inc(u_saved, 1)

                for g in range(NT * HEADS):
                    act.wait_ge(scores_ready, i * NT * HEADS + g + 1)
                    if g >= E_SLOTS:
                        act.wait_ge(probs_ready, i * NT * HEADS + g - E_SLOTS + 1)
                    elif tail:
                        act.wait_ge(probs1_ready, i * NT - (NT - 1 - g) % E_SLOTS)
                    act.activation(e_sb[:, g % E_SLOTS, :], ps[g % 2][:], ACT.Exp, scale=SCALE
                                   ).then_inc(exp_ready, 1)
                    if tail and g in TAIL_ACT:
                        second_end(i - 1, TAIL_ACT[g])
                    j, half = divmod(g - 2 * HEADS - LAG + 1, HEADS)
                    if j >= 0 and half < NH:
                        save_u(j, half)
                saved = max(0, NT * HEADS - 2 * HEADS - LAG + 1)
                for j in range(NT):
                    for half in range(NH):
                        if j * HEADS + half >= saved:
                            save_u(j, half)

            def layers(i, last):
                if not last:
                    save_xT(i + 1)
                rstd_of(i, 0, 1)
                if not last:
                    high_parts(i + 1)
                rstd_of(i, 1, 2)
                for half in range(NH):
                    s = slice(half * HALF, (half + 1) * HALF)
                    act.wait_ge(x1T_ps, i * 2 + half + 1)
                    act.activation(x1T[:, s], ps_u[:, s], ACT.Copy).then_inc(x1T_ready, 1)
                act.wait_ge(wh_ps, i + 1)
                act.activation(wh, ps[1][:], ACT.Copy).then_inc(wh_ready, 1)
                act.wait_ge(mrow_ps, i * 2 + 1)

                def exp1(t):
                    act.wait_ge(shifted, i * NT + t + 1)
                    act.activation(e_sb[:, t % E_SLOTS, :], e_sb[:, t % E_SLOTS, :], ACT.Exp
                                   ).then_inc(exp1_ready, 1)

                for t in range(NT):
                    if t >= E_SLOTS:
                        act.wait_ge(probs1_ready, i * NT + t - E_SLOTS + 1)
                    act.activation(e_sb[:, t % E_SLOTS, :], ps[0][:], ACT.Identity,
                                   bias=d_slope[:, t:t + 1]).then_inc(slope_ready, 1)
                    if t:
                        exp1(t - 1)
                exp1(NT - 1)

            def second_end(i, step):
                if step == "save":
                    act.wait_ge(h_ps, i * 2 + 2)
                    act.activation(hT, ps_u[:], ACT.Copy).then_inc(hT_ready, 1)
                elif step == "divide":
                    act.wait_ge(hp_ps, i + 1)
                    act.wait_ge(den_inv, i + 1)
                    for t in range(NT):
                        ins = act.activation(h1[:, t * P:(t + 1) * P], ps_u[:, t * P:(t + 1) * P],
                                             ACT.Identity, scale=den[:, t:t + 1])
                    ins.then_inc(h1_ready, 1)
                elif step == "elu":
                    act.wait_ge(h1_ready, i + 1)
                    act.activation(h_exp, h1, ACT.Relu, scale=-1.0).then_inc(act_chain, 1)
                    act.wait_ge(act_chain, i * ACT_CHAIN + 3)
                    act.activation(h_exp, h_exp, ACT.Exp, scale=-1.0).then_inc(elu_exp, 1)
                elif step == "rstd":
                    rstd_of(i, 2, 4)

            save_xT(0)
            high_parts(0)
            first_layer(0, False)
            with act.Fori(0, B - 1) as i:
                layers(i, False)
                first_layer(i + 1, True)
            layers(B - 1, True)
            for step in TAIL_ACT.values():
                second_end(B - 1, step)

        @block.tensor
        def _(pe):
            pe.wait_ge(consts, 10)
            pe.wait_ge(w_loaded, 12 * 16)
            for n in range(5):
                mm = pe.transpose(ps_u[:, n * F:(n + 1) * F], w_nat[:, n, :], ident[:])
            mm.then_inc(wT_ps, 1)
            for t in range(NT):
                pe.wait_ge(adj_cmp, 3 * t + 2)
                if t:
                    pe.wait_ge(adj_used, 2 * t)
                for m in range(2):
                    dst = ps[m][:].bitcast(BF16)
                    for c in range(NT):
                        mm = pe.transpose(dst[:, c * P:(c + 1) * P], adj_bf[m][:, c * P:(c + 1) * P],
                                          ident_bf[:])
                    mm.then_inc(adj_ps, 1)
            pe.wait_ge(wT_ready, 2)
            pe.wait_ge(out_stored, 16)
            pe.matmul(ps_small[:, 0:2], w_t[:, 4, :], a_sb[:], start=True, stop=True).then_inc(wa_ps, 1)
            pe.wait_ge(wa_ready, 1)
            pe.wait_ge(adj_used, 2 * NT)

            def queries_keys(i):
                pe.wait_ge(x_loaded, i * 16 + 16)
                for t in range(NT):
                    mm = pe.transpose(ps[0][:, t * P:(t + 1) * P], x_sb[:, t, :], ident[:])
                mm.then_inc(xT_ps, 1)
                pe.wait_ge(xT_ready, i + 1)
                for n, (dst, done) in enumerate(((ps[1], q_ps), (ps[0], k_ps))):
                    for half in range(NH):
                        s = slice(half * HALF, (half + 1) * HALF)
                        mm = pe.matmul(dst[:, s], w_t[:, n, :], xT[:, s], start=True, stop=True)
                    mm.then_inc(done, 1)

            def values(i):
                for t in range(NT):
                    mm = pe.matmul(ps_u[:, t * P:(t + 1) * P], xT[:, t * P:(t + 1) * P], w_t[:, 2, :],
                                   start=True, stop=True)
                mm.then_inc(v_ps, 1)

            def scores(i, j, h, tail):
                g = j * HEADS + h
                if g == 0:
                    if tail:
                        pe.wait_ge(slope_ready, i * NT)
                    else:
                        pe.wait_ge(lo_ready, i * 2 + 2)
                    pe.wait_ge(stacked, i * STACKS * 16 + STACKS * 16)
                elif g == 1:
                    if tail:
                        pe.wait_ge(shifted, i * NT)
                else:
                    pe.wait_ge(exp_ready, i * NT * HEADS + g - 1)
                for half in range(NH):
                    s = slice(half * HALF, (half + 1) * HALF)
                    mm = pe.matmul(ps[g % 2][:, s], k_st[:, h, j * P:(j + 1) * P], q_st[:, h, s],
                                   start=True, stop=True)
                mm.then_inc(scores_ready, 1)

            def first_layer(i, tail):
                def probs(j, h):
                    return p_sb[:, (j * HEADS + h) % P_SLOTS, :]

                def times_v(j, half):
                    if j:
                        pe.wait_ge(u_saved, i * NT * NH + (j - 1) * NH + half + 1)
                    elif half == 0:
                        pe.wait_ge(v_ready, i + 1)
                        if tail:
                            pe.wait_ge(h1_ready, i)
                    s = slice(half * HALF, (half + 1) * HALF)
                    for h in range(HEADS):
                        d = slice(h * DH, (h + 1) * DH)
                        mm = pe.matmul(ps_u[d, s], v_sb[:, j, d], probs(j, h)[:, s], start=True, stop=True)
                    mm.then_inc(u_ready, 1)

                def sums(j, quarters):
                    if quarters[0] == 0:
                        pe.wait_ge(probs_ready, i * NT * HEADS + (j + 1) * HEADS)
                    for c in quarters:
                        k = j * Q + c
                        for h in range(HEADS):
                            mm = pe.matmul(ps_sum[h * DH:(h + 1) * DH, 0:NQ],
                                           one_hot[:, DH - 1 - k:2 * DH - 1 - k],
                                           probs(j, h)[:, c * NQ:(c + 1) * NQ],
                                           start=(k == 0), stop=(k == NT * Q - 1),
                                           skip_group_check=True)
                    if k == NT * Q - 1:
                        mm.then_inc(sums_done, 1)

                for g in range(EARLY if tail else 0, NT * HEADS + HEADS + LAG):
                    if g < NT * HEADS:
                        scores(i, g // HEADS, g % HEADS, tail)
                    if tail and g in TAIL_PE:
                        second_end(i - 1)
                    j, piece = divmod(g - HEADS - LAG, HEADS)
                    if j >= 0 and piece < 2:
                        sums(j, (2 * piece, 2 * piece + 1))
                    elif j >= 0:
                        times_v(j, piece - 2)

            def layers(i, last):
                def project(n, half):
                    j = GROUPS[n][-1]
                    final = n == len(GROUPS) - 1
                    if half == 0 and n == 0:
                        pe.wait_ge(u_saved, (i + 1) * NT * NH)
                    if half == 0 or final:
                        pe.wait_ge(added, i * ADDS + adds_before(j + 1) + (half if final else 0))
                    for t in range(half * NT // 2, (half + 1) * NT // 2):
                        mm = pe.matmul(ps_u[:, t * P:(t + 1) * P], parts[n][:, t * P:(t + 1) * P],
                                       w_t[:, 3, :], start=(n == 0 and t == half * NT // 2),
                                       stop=final, skip_group_check=True)
                    if n == 0 and half == 1:
                        mm.then_inc(projected, 1)
                    if final:
                        mm.then_inc(o_ps, 1)

                pe.wait_ge(r_split, i + 1)
                pe.wait_ge(sel_ready, 1)
                pe.wait_ge(exp_ready, (i + 1) * NT * HEADS)
                todo = []
                for j in range(NT):
                    if j >= 2:
                        pe.wait_ge(u_scaled, i * NT + j - 1)
                    for c in range(Q):
                        for n in range(2):
                            mm = pe.matmul(ps[j % 2][:, c * NQ:(c + 1) * NQ], sel[:, j * Q + c, :],
                                           r_part[:, n, :], start=(n == 0), stop=(n == 1))
                    mm.then_inc(r_ps, 1)
                    for n, half in ((n, half) for n in range(len(GROUPS) - 1) for half in range(2)):
                        if j == min(GROUPS[n][-1] + 2 + half, NT - 1):
                            project(n, half)
                project(len(GROUPS) - 1, 0)
                project(len(GROUPS) - 1, 1)
                if not last:
                    queries_keys(i + 1)

                for half in range(NH):
                    pe.wait_ge(x1_ready, i * 2 + half + 1)
                    for t in range(half * NT // 2, (half + 1) * NT // 2):
                        mm = pe.transpose(ps_u[:, t * P:(t + 1) * P], x1[:, t, :], ident[:])
                    mm.then_inc(x1T_ps, 1)
                for half in range(NH):
                    pe.wait_ge(x1T_ready, i * 2 + half + 1)
                    s = slice(half * HALF, (half + 1) * HALF)
                    mm = pe.matmul(ps_rest[:, s], wa[:, 1:2].broadcast_to([P, P]), x1T[:, s],
                                   start=True, stop=True)
                mm.then_inc(drow_ps, 1)
                if not last:
                    pe.wait_ge(lo_ready, i * 2 + 4)
                for t in range(NT):
                    mm = pe.matmul(ps[0][:, 2 * t:2 * t + 2], x1T[:, t * P:(t + 1) * P], wa[:],
                                   start=True, stop=True)
                mm.then_inc(sd_ps, 1)
                for t in range(NT):
                    mm = pe.matmul(ps[1][:, t * P:(t + 1) * P], x1T[:, t * P:(t + 1) * P], w_nat[:, 4, :],
                                   start=True, stop=True)
                mm.then_inc(wh_ps, 1)
                if not last:
                    values(i + 1)
                pe.wait_ge(wh_ready, i + 1)
                for half in range(NH):
                    pe.wait_ge(m_ready, i * 2 + half + 1)
                    for n, dst in ((1, ps[0]), (0, ps[1])):
                        for t in range(half * NT // 2, (half + 1) * NT // 2):
                            mm = pe.transpose(dst[:, t * P:(t + 1) * P],
                                              u_cols[:, n, t:t + 1].broadcast_to([P, P]), ident[:])
                        if half:
                            mm.then_inc(mrow_ps, 1)
                if not last:
                    pe.wait_ge(v_ready, i + 2)

                def sums1(group):
                    for half in range(NH):
                        s = slice(half * HALF, (half + 1) * HALF)
                        for c in range(4):
                            mm = pe.matmul((ps_sum, ps_small)[half][c * DH:(c + 1) * DH, :], ones32[:],
                                           p_sb[:, 4 * group + c, s], start=(group == 0),
                                           stop=(group == 1), skip_group_check=True)
                    mm.then_inc(h_ps, 1)

                for t in range(NT):
                    if t == NT - 1 and not last:
                        for g in range(2):
                            scores(i + 1, 0, g, True)
                    pe.wait_ge(probs1_ready, i * NT + t + 1)
                    for half in range(NH):
                        s = slice(half * HALF, (half + 1) * HALF)
                        pe.matmul(ps_u[:, s], wh[:, t * P:(t + 1) * P], p_sb[:, t, s],
                                  start=(t == 0), stop=(t == NT - 1), skip_group_check=True)
                    if t == 3:
                        sums1(0)
                if not last:
                    for g in range(2, EARLY):
                        scores(i + 1, 0, g, True)
                sums1(1)

            def second_end(i):
                pe.wait_ge(den_ready, i * 2 + 2)
                for t in range(NT):
                    pe.matmul(ps_small[:, t:t + 1], den_sb[:, t * P:(t + 1) * P], quad_first[:],
                              start=True, stop=True)
                pe.wait_ge(hT_ready, i + 1)
                for t in range(NT):
                    mm = pe.transpose(ps_u[:, t * P:(t + 1) * P], hT[:, t * P:(t + 1) * P], ident[:])
                mm.then_inc(hp_ps, 1)

            queries_keys(0)
            values(0)
            first_layer(0, False)
            with pe.Fori(0, B - 1) as i:
                layers(i, False)
                first_layer(i + 1, True)
            layers(B - 1, True)
            second_end(B - 1)

        @block.vector
        def _(dve):
            dve.wait_ge(consts, 10)
            dve.wait_ge(adj_loaded, 16)
            for t in range(NT):
                a_t = u_sb[:, t, :].bitcast(I32)
                if t:
                    dve.wait_ge(adj_ps, 2 * t)
                    dve.wait_ge(adj_cmp, 3 * t)
                dve.tensor_scalar(adj_bf[0], a_t, 0.0, None, ALU.not_equal).then_inc(adj_cmp, 1)
                dve.tensor_scalar(adj_bf[1], a_t, 0.0, None, ALU.is_gt).then_inc(adj_cmp, 1)
                dve.wait_ge(adj_cmp, 3 * t + 2)
                dve.tensor_scalar(bias_n[:, t, :], adj_bf[1], -1.0, -NEG_BIG, ALU.add, ALU.mult
                                  ).then_inc(adj_cmp, 1)
                dve.wait_ge(adj_ps, 2 * (t + 1))
                q = slice(t * P, (t + 1) * P)
                for m, dst, a, b, op1 in ((0, clip_t, HI, LO, ALU.max), (1, keep_t, 255.0, 0.0, ALU.add)):
                    dve.tensor_scalar(dst[:, :, q],
                                      ps[m][:].bitcast(BF16)[:, 0:N].rearrange("p (c q) -> p c q", q=P),
                                      a, b, ALU.mult, op1).then_inc(adj_used, 1)
            dve.wait_ge(wa_ps, 1)
            dve.tensor_copy(wa[:], ps_small[:, 0:2]).then_inc(wa_ready, 1)

            def low_parts(i):
                for n, (src, hi, lo) in enumerate(((ps[1], q_hi, q_lo), (ps[0], k_hi, k_lo))):
                    dve.wait_ge(hi_ready, i * 2 + n + 1)
                    dve.scalar_tensor_tensor(out=lo, in0=src[:], scalar=bias_col[:, n:n + 1],
                                             in1=hi.bitcast(F32), op0=ALU.add, op1=ALU.subtract
                                             ).then_inc(lo_ready, 1)

            def values(i):
                dve.wait_ge(v_ps, i + 1)
                dve.tensor_tensor(v_sb[:], ps_u[:].rearrange("p (t f) -> p t f", f=F),
                                  rows[:, 0:1, :].broadcast_to([P, NT, F]), ALU.add).then_inc(v_ready, 1)

            def tiles(ap):
                return ap.rearrange("p (t f) -> p t f", f=F)

            HALF_TILES = (range(0, NT // 2), range(NT // 2, NT))

            def first_layer(i, end):
                for g in range(NT * HEADS):
                    j = g // HEADS
                    if g % HEADS == 0:
                        if j >= 2:
                            dve.wait_ge(u_ready, i * NT * NH + (j - 1) * NH)
                        elif end:
                            dve.wait_ge(h_ps, i * 2 - 1 + j)
                    dve.wait_ge(exp_ready, i * NT * HEADS + g + 1)
                    dve.scalar_tensor_tensor(out=p_sb[:, g % P_SLOTS, :], in0=e_sb[:, g % E_SLOTS, :],
                                             scalar=LO, in1=clip_t[:, j, :], op0=ALU.max,
                                             op1=ALU.min).then_inc(probs_ready, 1)
                    if end and g in TAIL_DVE:
                        end(TAIL_DVE[g])

            def layers(i, last):
                steps = [0]

                def mark(ins):
                    steps[0] += 1
                    ins.then_inc(dve_chain, 1)
                    return steps[0]

                def need(step):
                    dve.wait_ge(dve_chain, i * DVE_CHAIN + step)

                def chain(ins):
                    need(mark(ins))

                def take_stats(src, which):
                    for t in which:
                        ins = dve.bn_stats(stats[:, t, :], src[:, t, :])
                    return ins

                def variance():
                    dve.tensor_tensor(halves[:, 0, :], stats[:, :, 1], stats[:, :, 4], ALU.add)
                    step = mark(dve.tensor_tensor(halves[:, 1, :], stats[:, :, 1], stats[:, :, 4],
                                                  ALU.subtract))
                    dve.tensor_tensor(halves[:, 2, :], stats[:, :, 2], stats[:, :, 5], ALU.add)
                    need(step)
                    dve.tensor_tensor(halves[:, 3, :], halves[:, 1, :], halves[:, 1, :], ALU.mult)
                    chain(dve.tensor_scalar(mean[:], halves[:, 0, :], 0.5, None, ALU.mult))
                    dve.scalar_tensor_tensor(out=f_var[:], in0=halves[:, 3, :], scalar=F / 4,
                                             in1=halves[:, 2, :], op0=ALU.mult, op1=ALU.add
                                             ).then_inc(var_ready, 1)

                def normalise(src, dst, which):
                    for t in which:
                        ins = dve.tensor_scalar(dst[:, t, :], src[:, t, :], mean[:, t:t + 1],
                                                rstd_col[:, t:t + 1], ALU.subtract, ALU.mult)
                    return ins

                dve.wait_ge(sums_done, i + 1)
                chain(dve.reciprocal(r_sb, ps_sum[:, 0:NQ]))
                chain(dve.tensor_copy(r_part[:, 0, :], r_sb))
                dve.tensor_tensor(r_part[:, 1, :], r_sb, r_part[:, 0, :].bitcast(F32), ALU.subtract
                                  ).then_inc(r_split, 1)
                dve.wait_ge(u_saved, (i + 1) * NT * NH)
                starts = {g[0]: n for n, g in enumerate(GROUPS)}
                group_of = {j: n for n, g in enumerate(GROUPS) for j in g}

                def add(j):
                    n = group_of[j]
                    dve.wait_ge(u_scaled, i * NT + j + 1)
                    if j - 1 not in starts:
                        dve.wait_ge(added, i * ADDS + adds_before(j))
                    for s in (slice(0, N),) if j < NT - 1 else (slice(0, HALF), slice(HALF, N)):
                        dve.tensor_tensor(parts[n][:, s], parts[n][:, s], u_sb[:, j, s], ALU.add
                                          ).then_inc(added, 1)

                for j in range(NT):
                    if j in starts and starts[j] == len(GROUPS) - 1:
                        dve.wait_ge(projected, i + 1)
                    dve.wait_ge(r_ps, i * NT + j + 1)
                    dst = parts[starts[j]] if j in starts else u_sb[:, j, :]
                    dve.tensor_tensor(dst, u_sb[:, j, :], ps[j % 2][:], ALU.mult).then_inc(u_scaled, 1)
                    if j and j - 1 not in starts:
                        add(j - 1)
                add(NT - 1)
                dve.wait_ge(xb_ready, i * 2 + 2)
                for half in range(NH):
                    s = slice(half * HALF, (half + 1) * HALF)
                    dve.wait_ge(o_ps, i * 2 + half + 1)
                    step = mark(dve.tensor_tensor(y0[:, s], ps_u[:, s], xb[:, s], ALU.add))
                    if half:
                        take_stats(tiles(y0), HALF_TILES[0])
                    else:
                        first = step
                        need(first)
                need(step)
                chain(take_stats(tiles(y0), HALF_TILES[1]))
                variance()
                for t in range(NT):
                    ins = dve.scalar_tensor_tensor(out=tiles(g0)[:, t, :], in0=tiles(y0)[:, t, :],
                                                   scalar=mean[:, t:t + 1], in1=rows[:, 2, :],
                                                   op0=ALU.subtract, op1=ALU.mult)
                chain(ins)
                dve.wait_ge(rstd_ready, i * 3 + 1)
                done = []
                for which in HALF_TILES:
                    for t in which:
                        ins = dve.scalar_tensor_tensor(out=tiles(z0)[:, t, :], in0=tiles(g0)[:, t, :],
                                                       scalar=rstd_col[:, t:t + 1],
                                                       in1=tiles(x_beta)[:, t, :],
                                                       op0=ALU.mult, op1=ALU.add)
                    done.append(mark(ins))
                need(done[0])
                take_stats(tiles(z0), HALF_TILES[0])
                need(done[1])
                chain(take_stats(tiles(z0), HALF_TILES[1]))
                variance()
                dve.wait_ge(rstd_ready, i * 3 + 2)
                for which in HALF_TILES:
                    normalise(tiles(z0), x1, which).then_inc(x1_ready, 1)
                if not last:
                    low_parts(i + 1)

                dve.wait_ge(drow_ps, i + 1)
                dve.wait_ge(sd_ps, i + 1)
                dve.tensor_copy(sd_col[:].rearrange("p t c -> p (t c)"), ps[0][:, 0:2 * NT]
                                ).then_inc(sd_ready, 1)
                for half, which in enumerate(HALF_TILES):
                    w = slice(which[0], which[-1] + 1)
                    for t in which:
                        ins = dve.tensor_tensor_reduce(p_sb[:, t, :], ps_rest[:], bias_n[:, t, :], 1.0,
                                                       NEG_BIG, ALU.add, ALU.max, row_max[:, t:t + 1])
                    chain(ins)
                    if half == 0:
                        dve.wait_ge(sd_ready, i + 1)
                    step = mark(dve.tensor_tensor(m_tmp[:, w], row_max[:, w], sd_col[:, w, 0], ALU.add))
                    dve.tensor_scalar(d_slope[:, w], sd_col[:, w, 1], NEG_SLOPE, None, ALU.mult)
                    need(step)
                    chain(dve.scalar_tensor_tensor(out=m_col[:, w], in0=m_tmp[:, w], scalar=NEG_SLOPE,
                                                   in1=m_tmp[:, w], op0=ALU.mult, op1=ALU.max))
                    dve.tensor_tensor(u_cols[:, 0, w], sd_col[:, w, 0], m_col[:, w], ALU.subtract)
                    dve.scalar_tensor_tensor(out=u_cols[:, 1, w], in0=sd_col[:, w, 0], scalar=NEG_SLOPE,
                                             in1=m_col[:, w], op0=ALU.mult, op1=ALU.subtract
                                             ).then_inc(m_ready, 1)
                if not last:
                    values(i + 1)
                dve.wait_ge(mrow_ps, i * 2 + 2)

                def mask1(t):
                    dve.wait_ge(exp1_ready, i * NT + t + 1)
                    dve.tensor_tensor(p_sb[:, t, :], e_sb[:, t % E_SLOTS, :], keep_t[:, t, :], ALU.min
                                      ).then_inc(probs1_ready, 1)

                for t in range(NT):
                    dve.wait_ge(slope_ready, i * NT + t + 1)
                    dve.scalar_tensor_tensor(out=e_sb[:, t % E_SLOTS, :], in0=ps[1][:],
                                             scalar=sd_col[:, t, 1:2], in1=e_sb[:, t % E_SLOTS, :],
                                             op0=ALU.add, op1=ALU.max).then_inc(shifted, 1)
                    if t:
                        mask1(t - 1)
                mask1(NT - 1)

                left = {}

                def end(step):
                    if step == "den":
                        dve.wait_ge(h_ps, i * 2 + 2)
                        dve.tensor_copy(den_sb[:, 0:HALF], ps_sum).then_inc(den_ready, 1)
                        dve.tensor_copy(den_sb[:, HALF:N], ps_small).then_inc(den_ready, 1)
                    elif step == "inverse":
                        dve.wait_ge(hp_ps, i + 1)
                        dve.reciprocal(den[:], ps_small[:, 0:NT]).then_inc(den_inv, 1)
                    elif step == "residual":
                        dve.wait_ge(h1_ready, i + 1)
                        left["z1"] = mark(dve.scalar_tensor_tensor(
                            out=tiles(z1), in0=tiles(h1), scalar=0.0, in1=x1[:], op0=ALU.max,
                            op1=ALU.add))
                    elif step == "elu":
                        need(left["z1"])
                        dve.wait_ge(elu_exp, i + 1)
                        left["h1"] = mark(dve.scalar_tensor_tensor(
                            out=h1, in0=h_exp, scalar=-1.0, in1=z1, op0=ALU.add, op1=ALU.add))
                    elif step == "stats0":
                        need(left["h1"])
                        take_stats(tiles(h1), HALF_TILES[0])
                    elif step == "stats1":
                        left["stats"] = mark(take_stats(tiles(h1), HALF_TILES[1]))
                    elif step == "variance":
                        need(left["stats"])
                        variance()
                    elif step == "out0":
                        dve.wait_ge(rstd_ready, i * 3 + 3)
                        normalise(tiles(h1), tiles(out_sb), HALF_TILES[0])
                    elif step == "out1":
                        normalise(tiles(h1), tiles(out_sb), HALF_TILES[1]).then_inc(out_ready, 1)
                        assert steps[0] == DVE_CHAIN, steps
                return end

            low_parts(0)
            values(0)
            first_layer(0, None)
            with dve.Fori(0, B - 1) as i:
                first_layer(i + 1, layers(i, False))
            end = layers(B - 1, True)
            for step in TAIL_DVE.values():
                end(step)


_INS = ["x", "adj", "L0_gnn_Wq", "L0_gnn_bq", "L0_gnn_Wk", "L0_gnn_bk", "L0_gnn_Wv", "L0_gnn_bv",
        "L0_gnn_Wo", "L0_gnn_bo", "L0_gnn_gamma", "L0_gnn_beta", "L1_gnn_W", "L1_gnn_a"]


def kernel(**inputs):
    import numpy as _np
    import concourse.bacc as _bacc
    from concourse import mybir as _mybir
    from concourse.bass_utils import run_bass_kernel_spmd as _run

    nc = _bacc.Bacc("TRN2", target_bir_lowering=False, num_devices=1)
    arrays, args = {}, []
    for name in _INS:
        a = _np.ascontiguousarray(inputs[name])
        arrays[f"in_{name}"] = a
        args.append(nc.dram_tensor(f"in_{name}", a.shape, _mybir.dt.from_np(a.dtype),
                                   kind="ExternalInput").ap())
    shape = tuple(inputs["x"].shape)
    args.append(nc.dram_tensor("out_dram", shape, _mybir.dt.from_np(_np.dtype("float32")),
                               kind="ExternalOutput").ap())
    build(nc, *args)
    r = _run(nc, [arrays], core_ids=[0])
    return r.results[0]["out_dram"]
```

```python
import math
from contextlib import ExitStack

import numpy as np

import concourse.bass as bass
from concourse import mybir

F32 = mybir.dt.float32
F32R = mybir.dt.float32r
BF16 = mybir.dt.bfloat16
U8 = mybir.dt.uint8
I32 = mybir.dt.int32
ALU = mybir.AluOpType
ACT = mybir.ActivationFunctionType

P = 128
HEADS = 4
SCORE_CLIP = 10.0
NEG_SLOPE = 0.2
LN_EPS = 1e-5
TINY = 1e-30
NEG_BIG = -1e30


def build(nc, x, adj, Wq, bq, Wk, bk, Wv, bv, Wo, bo, gamma, beta, W1, a1, out):
    B, N, F = x.shape
    assert F == P and N % P == 0
    NT = N // P
    DH = F // HEADS
    HALF = 512
    NH = N // HALF
    Q = 4
    NQ = N // Q
    assert NT * Q == DH and NT == 8
    SCALE = 1.0 / math.sqrt(DH)
    LO = float(np.exp(np.float32(-SCORE_CLIP)))
    HI = float(np.exp(np.float32(SCORE_CLIP)))
    E_SLOTS = 3
    LAG = 2
    P_SLOTS = 2 * HEADS
    SLOTS = P_SLOTS + E_SLOTS
    SEL_ROWS = NT * Q * P // N
    EARLY = 4
    CUT = 6
    GROUPS = ((0, 1), (2, 3), (4, 5), (6, 7))

    with ExitStack() as ctx:
        def sb(name, shape, dt=F32):
            return ctx.enter_context(nc.sbuf_tensor(name, shape, dt))

        def sem(name):
            return ctx.enter_context(nc.semaphore(name))

        ident = sb("ident", [P, P])
        ident_bf = sb("ident_bf", [P, P], BF16)
        ones32 = sb("ones32", [P, DH])
        one_hot = sb("one_hot", [P, 2 * DH - 1])
        sel = sb("sel", [P, NT * Q, P], F32R)
        quad_first = sb("quad_first", [P, 1])
        w1_nat = sb("w1_nat", [P, F])
        w_t = sb("w_t", [P, 4, F])
        bias_col = sb("bias_col", [P, 3])
        rows = sb("rows", [P, 3, F])
        a_sb = sb("a_sb", [P, 2])
        wa = sb("wa", [P, 2])
        wa_row = sb("wa_row", [P, F])
        eps_col = sb("eps_col", [P, 1])
        lo_col = sb("lo_col", [P, 1])
        clip_t = sb("clip_t", [P, NT, N])
        keep_t = sb("keep_t", [P, NT, N], U8)
        bias_n = sb("bias_n", [P, NT, N], BF16)
        x_sb = sb("x_sb", [P, NT, F])
        xT = sb("xT", [P, N])
        k_st = sb("k_st", [P, HEADS, N], F32R)
        q_st = sb("q_st", [P, HEADS, N], F32R)
        v_sb = sb("v_sb", [P, NT, F])
        e_sb = sb("e_sb", [P, E_SLOTS, N])
        p_sb = sb("p_sb", [P, P_SLOTS, N])
        u_sb = sb("u_sb", [P, NT, N])
        r_sb = sb("r_sb", [P, NQ])
        r_part = sb("r_part", [P, 2, 2, NQ], F32R)
        x1 = sb("x1", [P, NT, F])
        stats = sb("stats", [P, NT, 6])
        halves = sb("halves", [P, 4, NT])
        mean = sb("mean", [P, NT])
        f_var = sb("f_var", [P, NT])
        ln_var = sb("ln_var", [P, NT])
        rstd_col = sb("rstd_col", [P, NT])
        dst_col = sb("dst_col", [P, NT])
        sd_col = sb("sd_col", [P, NT, 2])
        row_max = sb("row_max", [P, NT])
        m_col = sb("m_col", [P, NT])
        u_cols = sb("u_cols", [P, 2, NT])
        d_slope = sb("d_slope", [P, NT])
        m_tmp = sb("m_tmp", [P, NT])
        den = sb("den", [P, NT])
        shift_col = m_tmp
        q_hi = u_sb[:, 0, :].bitcast(F32R)
        q_lo = u_sb[:, 1, :].bitcast(F32R)
        k_hi = u_sb[:, 2, :].bitcast(F32R)
        k_lo = u_sb[:, 3, :].bitcast(F32R)
        adj_i = [(u_sb if t < 4 else p_sb)[:, 4 + t % 4, :].bitcast(I32) for t in range(NT)]
        adj_bf = [[p_sb[:, 2 * n + m, 0:N // 2].bitcast(BF16) for m in range(2)] for n in range(2)]
        sel_flat = clip_t[:, 0:SEL_ROWS, :]
        w_nat = [xT[:, n * F:(n + 1) * F] for n in range(4)] + [w1_nat[:]]
        w1_t = e_sb[:, 0, 0:F]
        x1T = u_sb[:, 4, :]
        wh = u_sb[:, 5, :]

        def slot(g):
            n = (P_SLOTS + g) % SLOTS
            return p_sb[:, n, :] if n < P_SLOTS else e_sb[:, n - P_SLOTS, :]

        parts = [p_sb[:, n, :] for n in (0, 1, 2, 7)]
        xb = p_sb[:, 4, :]
        x_beta = p_sb[:, 5, :]
        y0 = p_sb[:, 6, :]
        g0 = p_sb[:, 3, :]
        z0 = p_sb[:, 0, :]
        hT = u_sb[:, 4, :]
        h_exp = u_sb[:, 5, :]
        h1 = u_sb[:, 6, :]
        den_sb = u_sb[:, 7, :]
        z1 = u_sb[:, 7, :]
        out_sb = u_sb[:, 7, :]

        ps = [ctx.enter_context(nc.psum_tensor(f"ps{n}", [P, N], F32)) for n in range(2)]
        ps_u = ctx.enter_context(nc.psum_tensor("ps_u", [P, N], F32))
        ps_rest = ctx.enter_context(nc.psum_tensor("ps_rest", [P, N], F32))
        ps_sum = ps_rest[:, 0:HALF]
        ps_small = ps_rest[:, HALF:N]

        def adj_t(m, t):
            return ps_rest[:, m * HALF:(m + 1) * HALF].bitcast(BF16)

        chunk_sums = (ps_sum[:, 0:NQ], ps_small[:, 0:NQ])

        w_loaded = sem("w_loaded")
        b_loaded = sem("b_loaded")
        adj_loaded = [sem(f"adj_loaded{t}") for t in range(NT)]
        ident_ready = sem("ident_ready")
        memsets = sem("memsets")
        consts = sem("consts")
        sel_ready = sem("sel_ready")
        adj_cmp = sem("adj_cmp")
        adj_ps = sem("adj_ps")
        clip_made = sem("clip_made")
        keep_act = sem("keep_act")
        keep_dve = sem("keep_dve")
        wT_ps = sem("wT_ps")
        wT_ready = sem("wT_ready")
        wa_ps = sem("wa_ps")
        wa_ready = sem("wa_ready")
        bo_ready = sem("bo_ready")
        x_loaded = sem("x_loaded")
        xT_ps = sem("xT_ps")
        xT_ready = sem("xT_ready")
        q_ps = sem("q_ps")
        k_ps = sem("k_ps")
        v_ps = sem("v_ps")
        hi_ready = sem("hi_ready")
        lo_ready = sem("lo_ready")
        v_ready = sem("v_ready")
        q_stacked = sem("q_stacked")
        k_stacked = [sem(f"k_stacked{h}") for h in range(HEADS)]
        scores_ready = sem("scores_ready")
        exp_ready = sem("exp_ready")
        probs_ready = sem("probs_ready")
        u_ready = sem("u_ready")
        u_saved = sem("u_saved")
        sums_done = sem("sums_done")
        r_chain = sem("r_chain")
        r_split = sem("r_split")
        r_ps = sem("r_ps")
        u_scaled = sem("u_scaled")
        added = sem("added")
        o_ps = sem("o_ps")
        xb_ready = sem("xb_ready")
        var_ready = sem("var_ready")
        rstd_ready = sem("rstd_ready")
        act_chain = sem("act_chain")
        dve_chain = sem("dve_chain")
        shift_ready = sem("shift_ready")
        x1_ready = sem("x1_ready")
        x1_more = sem("x1_more")
        x1T_ps = sem("x1T_ps")
        x1T_ready = sem("x1T_ready")
        wh_ps = sem("wh_ps")
        dst_ready = sem("dst_ready")
        drow_ps = sem("drow_ps")
        sd_ps = sem("sd_ps")
        wh_ready = sem("wh_ready")
        m_ready = sem("m_ready")
        mrow_ps = sem("mrow_ps")
        slope_ready = sem("slope_ready")
        shifted = sem("shifted")
        exp1_ready = sem("exp1_ready")
        probs1_ready = sem("probs1_ready")
        h_ps = sem("h_ps")
        hT_ready = sem("hT_ready")
        den_ready = sem("den_ready")
        den_ps = sem("den_ps")
        hp_ps = sem("hp_ps")
        den_inv = sem("den_inv")
        h1_ready = sem("h1_ready")
        elu_exp = sem("elu_exp")
        out_ready = sem("out_ready")
        out_stored = sem("out_stored")

        ADDS = sum(len(g) - 1 for g in GROUPS) + 1
        DVE_CHAIN = 22
        ACT_CHAIN = 4

        def adds_before(j):
            return sum(1 for g in GROUPS for c in g[1:] if c < j)

        TAIL_PE = {4: "turn", 6: "den"}
        TAIL_ACT = {3: "save", 7: "divide", 9: "elu", 19: "rstd"}
        TAIL_DVE = {3: "den", 6: "inverse", 9: "residual", 11: "elu", 13: "stats0", 15: "stats1",
                    17: "variance", 21: "out0", 23: "out1"}
        HELD = {6: (), 8: (6, 7, 8), 10: (9, 10, 11)}
        DVE_KEEPS = (0, 2, 4, 6)
        MAX_TILES = (range(0, 6), range(6, NT))

        block = ctx.enter_context(nc.Block())

        @block.sync
        def _(sp):
            sp.dma_start(x_sb[:], x[0].rearrange("(t p) f -> p t f", p=P)).then_inc(x_loaded, 16)
            for n, w in enumerate((Wq, Wk, Wv, Wo, W1)):
                sp.dma_start(w_nat[n], w).then_inc(w_loaded, 16)
            sp.dma_start(a_sb[:, 0:1], a1[0:P, :]).then_inc(b_loaded, 16)
            sp.dma_start(a_sb[:, 1:2], a1[P:2 * P, :]).then_inc(out_stored, 16)
            for t in range(NT):
                sp.dma_start(adj_i[t], adj[t * P:(t + 1) * P, :]).then_inc(adj_loaded[t], 16)

            def stack(i):
                def copies(st, src, quad, h, done):
                    sp.dma_start(st[quad * DH:(quad + 1) * DH, h, :].bitcast(F32),
                                 src[h * DH:(h + 1) * DH, :].bitcast(F32)).then_inc(done, 16)

                for src, quads, done in ((q_hi, (0, 2), hi_ready), (q_lo, (1, 3), lo_ready)):
                    sp.wait_ge(done, i * 2 + 1)
                    for quad in quads:
                        for h in range(HEADS):
                            copies(q_st, src, quad, h, q_stacked)
                sp.wait_ge(hi_ready, i * 2 + 2)
                sp.wait_ge(lo_ready, i * 2 + 2)
                for h in range(HEADS):
                    for quad in range(4):
                        copies(k_st, k_hi if quad < 2 else k_lo, quad, h, k_stacked[h])

            def batch(i, last):
                if not last:
                    sp.wait_ge(xb_ready, i * 2 + 2)
                    sp.dma_start(x_sb[:], x[bass.ds(i + 1, 1)].rearrange("a (t p) f -> p (a t) f", p=P)
                                 ).then_inc(x_loaded, 16)
                    stack(i + 1)
                sp.wait_ge(out_ready, i + 1)
                sp.dma_start(out[bass.ds(i, 1)].rearrange("a (t p) f -> p (a t) f", p=P),
                             out_sb.rearrange("p (t f) -> p t f", f=F)).then_inc(out_stored, 16)

            stack(0)
            with sp.Fori(0, B - 1) as i:
                batch(i, False)
            batch(B - 1, True)
            sp.wait_ge(out_stored, 16 * B + 16)

        @block.gpsimd
        def _(pool):
            pool.memset(ident[:], 0.0).then_inc(memsets, 1)
            pool.memset(ident_bf[:], 0.0).then_inc(memsets, 1)
            pool.wait_ge(memsets, 2)
            for m in (ident, ident_bf):
                pool.affine_select(out=m[:], in_=m[:], compare_op=ALU.not_equal, fill=1.0, base=0,
                                   pattern=[[-1, P]], channel_multiplier=1).then_inc(ident_ready, 1)
            pool.memset(eps_col[:], LN_EPS).then_inc(consts, 1)
            pool.memset(lo_col[:], LO).then_inc(consts, 1)
            pool.memset(ones32[:], 1.0).then_inc(consts, 1)
            pool.memset(quad_first[:], 0.0).then_inc(memsets, 1)
            pool.memset(one_hot[:], 0.0).then_inc(memsets, 1)
            pool.memset(sel_flat, 0.0).then_inc(memsets, 1)
            pool.wait_ge(memsets, 5)
            pool.memset(one_hot[:, DH - 1:DH], 1.0).then_inc(consts, 1)
            sel_v = sel_flat.rearrange("p a (k h d) -> p (a k) h d", h=HEADS, d=DH)
            pool.affine_select(out=sel_v, in_=sel_v, compare_op=ALU.not_equal, fill=1.0, base=0,
                               pattern=[[-1, NT * Q], [-DH, HEADS], [0, DH]], channel_multiplier=1
                               ).then_inc(consts, 1)
            for h in range(HEADS):
                pool.wait_ge(consts, 5 + h)
                pool.memset(quad_first[h * DH:h * DH + 1, :], 1.0).then_inc(consts, 1)
            pool.wait_ge(bo_ready, 1)

            def batch(i):
                pool.wait_ge(x_loaded, i * 16 + 16)
                pool.wait_ge(u_ready, (i + 1) * NT * NH)
                for dst, row in ((xb, 0), (x_beta, 2)):
                    pool.tensor_tensor(dst.rearrange("p (t f) -> p t f", f=F), x_sb[:],
                                       rows[:, row:row + 1, :].broadcast_to([P, NT, F]), ALU.add
                                       ).then_inc(xb_ready, 1)

            with pool.Fori(0, B) as i:
                batch(i)

        @block.scalar
        def _(act):
            for n, b in enumerate((bq, bk, bv)):
                act.dma_start(bias_col[:, n:n + 1], b.rearrange("(p o) -> p o", o=1)).then_inc(b_loaded, 16)
            for n, b in enumerate((bo, gamma, beta)):
                act.dma_start(rows[:, n, :], b.rearrange("(o f) -> o f", o=1).broadcast_to([P, F])
                              ).then_inc(b_loaded, 16)
            act.preload_act_table_set("natural_log_exp_and_others")
            act.wait_ge(wT_ps, 1)
            act.activation(w_t[:, 0:4, :].rearrange("p a f -> p (a f)"), ps_u[:, 0:4 * F], ACT.Copy
                           ).then_inc(wT_ready, 1)
            act.activation(w1_t, ps_u[:, 4 * F:5 * F], ACT.Copy).then_inc(wT_ready, 1)

            def rstd_of(i, k, step):
                act.wait_ge(var_ready, i * 3 + k + 1)
                act.activation(ln_var[:], f_var[:], ACT.Ln, bias=eps_col[:], scale=1.0 / F
                               ).then_inc(act_chain, 1)
                act.wait_ge(act_chain, i * ACT_CHAIN + step)
                act.activation(rstd_col[:], ln_var[:], ACT.Exp, scale=-0.5).then_inc(rstd_ready, 1)

            def save_xT(i):
                act.wait_ge(xT_ps, i + 1)
                act.activation(xT[:], ps[0][:], ACT.Copy).then_inc(xT_ready, 1)

            def high_parts(i):
                act.wait_ge(q_ps, i + 1)
                act.activation(q_hi, ps[1][:], ACT.Identity, bias=bias_col[:, 0:1]).then_inc(hi_ready, 1)
                act.wait_ge(k_ps, i + 1)
                act.activation(k_hi, ps[0][:], ACT.Identity, bias=bias_col[:, 1:2]).then_inc(hi_ready, 1)

            def save_v(i, src):
                act.wait_ge(v_ps, i + 1)
                act.activation(v_sb[:].rearrange("p t f -> p (t f)"), src[:], ACT.Copy
                               ).then_inc(v_ready, 1)

            def first_layer(i, tail):
                def save_u(j, half):
                    act.wait_ge(u_ready, i * NT * NH + j * NH + half + 1)
                    if half == 0:
                        if j == 5 and tail:
                            act.wait_ge(out_ready, i)
                        elif j == NT - 1:
                            act.wait_ge(out_stored, i * 16 + 16)
                    act.activation(u_sb[:, j, half * HALF:(half + 1) * HALF],
                                   ps_u[:, half * HALF:(half + 1) * HALF], ACT.Copy).then_inc(u_saved, 1)

                for g in range(NT * HEADS):
                    act.wait_ge(scores_ready, i * NT * HEADS + g + 1)
                    if g >= SLOTS:
                        act.wait_ge(u_ready, i * NT * NH + ((g - SLOTS) // HEADS + 1) * NH)
                    elif tail and g < E_SLOTS:
                        act.wait_ge(probs1_ready, i * NT - (NT - 1 - g) % E_SLOTS)
                    elif tail:
                        act.wait_ge(h_ps, i * 2 - int(g < E_SLOTS + P_SLOTS // 2))
                    act.activation(slot(g), ps[g % 2][:], ACT.Exp, scale=SCALE
                                   ).then_inc(exp_ready, 1)
                    if tail and g in TAIL_ACT:
                        second_end(i - 1, TAIL_ACT[g])
                    j, half = divmod(g - 2 * HEADS - LAG + 1, HEADS)
                    if j >= 0 and half < NH:
                        save_u(j, half)
                saved = max(0, NT * HEADS - 2 * HEADS - LAG + 1)
                for j in range(NT):
                    for half in range(NH):
                        if j * HEADS + half >= saved:
                            save_u(j, half)

            def layers(i, last):
                if not last:
                    save_xT(i + 1)
                rstd_of(i, 0, 1)
                if not last:
                    high_parts(i + 1)
                rstd_of(i, 1, 2)
                act.wait_ge(shift_ready, i + 1)
                for t in range(NT // 2, NT):
                    ins = act.activation(x1[:, t, :], z0[:, t * P:(t + 1) * P], ACT.Identity,
                                         bias=shift_col[:, t:t + 1], scale=rstd_col[:, t:t + 1])
                ins.then_inc(x1_more, 1)
                for half in range(NH):
                    s = slice(half * HALF, (half + 1) * HALF)
                    act.wait_ge(x1T_ps, i * 2 + half + 1)
                    act.activation(x1T[:, s], ps_u[:, s], ACT.Copy).then_inc(x1T_ready, 1)
                act.wait_ge(wh_ps, i + 1)
                act.activation(wh, ps[1][:], ACT.Copy).then_inc(wh_ready, 1)

                def exp1(t):
                    act.wait_ge(shifted, i * NT + t + 1)
                    act.activation(e_sb[:, t % E_SLOTS, :], e_sb[:, t % E_SLOTS, :], ACT.Exp
                                   ).then_inc(exp1_ready, 1)

                for t in range(NT):
                    if t >= E_SLOTS:
                        act.wait_ge(probs1_ready, i * NT + t - E_SLOTS + 1)
                    for n, which in enumerate(((0, HALF), (HALF, N)) if t == 0 else ((0, N),)):
                        s = slice(*which)
                        if t == 0:
                            act.wait_ge(mrow_ps, i * 3 + n + 1)
                        ins = act.activation(e_sb[:, t % E_SLOTS, s], ps[0][:, s], ACT.Identity,
                                             bias=d_slope[:, t:t + 1])
                    ins.then_inc(slope_ready, 1)
                    if t:
                        exp1(t - 1)
                    if t == 2 and not last:
                        save_v(i + 1, ps_rest)
                exp1(NT - 1)

            def second_end(i, step):
                if step == "save":
                    act.wait_ge(h_ps, i * 2 + 2)
                    act.activation(hT, ps_u[:], ACT.Copy).then_inc(hT_ready, 1)
                elif step == "divide":
                    act.wait_ge(hp_ps, i + 1)
                    act.wait_ge(den_inv, i + 1)
                    for t in range(NT):
                        ins = act.activation(h1[:, t * P:(t + 1) * P], ps_u[:, t * P:(t + 1) * P],
                                             ACT.Identity, scale=den[:, t:t + 1])
                    ins.then_inc(h1_ready, 1)
                elif step == "elu":
                    act.wait_ge(h1_ready, i + 1)
                    act.activation(h_exp, h1, ACT.Relu, scale=-1.0).then_inc(act_chain, 1)
                    act.wait_ge(act_chain, i * ACT_CHAIN + 3)
                    act.activation(h_exp, h_exp, ACT.Exp, scale=-1.0).then_inc(elu_exp, 1)
                elif step == "rstd":
                    rstd_of(i, 2, 4)

            save_xT(0)
            act.wait_ge(consts, 5 + HEADS)
            act.activation(sel[:].rearrange("p k m -> p (k m)"),
                           sel_flat.rearrange("p a c -> p (a c)"), ACT.Copy).then_inc(sel_ready, 1)
            act.wait_ge(b_loaded, 7 * 16)
            high_parts(0)
            save_v(0, ps_u)
            act.wait_ge(sel_ready, 1)
            for t in range(NT):
                q = slice(t * P, (t + 1) * P)
                for m, dst, bias, scale in ((0, clip_t, lo_col[:], HI), (1, keep_t, 0.0, 255.0)):
                    if m and t in DVE_KEEPS:
                        continue
                    act.wait_ge(adj_ps, 2 * t + m + 1)
                    act.activation(dst[:, :, q], adj_t(m, t).rearrange("p (c q) -> p c q", q=P),
                                   ACT.Identity, bias=bias, scale=scale
                                   ).then_inc(keep_act if m else clip_made, 1)
            act.wait_ge(adj_cmp, 3 * NT)
            first_layer(0, False)
            with act.Fori(0, B - 1) as i:
                layers(i, False)
                first_layer(i + 1, True)
            layers(B - 1, True)
            for step in TAIL_ACT.values():
                second_end(B - 1, step)

        @block.tensor
        def _(pe):
            pe.wait_ge(ident_ready, 2)
            pe.wait_ge(w_loaded, 5 * 16)
            for n in range(5):
                mm = pe.transpose(ps_u[:, n * F:(n + 1) * F], w_nat[n], ident[:])
            mm.then_inc(wT_ps, 1)

            def turn_x(i):
                pe.wait_ge(x_loaded, i * 16 + 16)
                for t in range(NT):
                    mm = pe.transpose(ps[0][:, t * P:(t + 1) * P], x_sb[:, t, :], ident[:])
                mm.then_inc(xT_ps, 1)

            def queries_keys(i):
                pe.wait_ge(xT_ready, i + 1)
                for n, (dst, done) in enumerate(((ps[1], q_ps), (ps[0], k_ps))):
                    for half in range(NH):
                        s = slice(half * HALF, (half + 1) * HALF)
                        mm = pe.matmul(dst[:, s], w_t[:, n, :], xT[:, s], start=True, stop=True)
                    mm.then_inc(done, 1)

            def values(i, dst):
                for t in range(NT):
                    mm = pe.matmul(dst[:, t * P:(t + 1) * P], xT[:, t * P:(t + 1) * P], w_t[:, 2, :],
                                   start=True, stop=True)
                mm.then_inc(v_ps, 1)

            def scores(i, j, h, tail):
                g = j * HEADS + h
                if g == 0:
                    if tail:
                        pe.wait_ge(slope_ready, i * NT)
                    else:
                        pe.wait_ge(lo_ready, i * 2 + 2)
                    pe.wait_ge(q_stacked, i * 4 * HEADS * 16 + 4 * HEADS * 16)
                elif g == 1:
                    if tail:
                        pe.wait_ge(shifted, i * NT)
                else:
                    pe.wait_ge(exp_ready, i * NT * HEADS + g - 1)
                if j == 0:
                    pe.wait_ge(k_stacked[h], i * 4 * 16 + 4 * 16)
                for half in range(NH):
                    s = slice(half * HALF, (half + 1) * HALF)
                    mm = pe.matmul(ps[g % 2][:, s], k_st[:, h, j * P:(j + 1) * P], q_st[:, h, s],
                                   start=True, stop=True)
                mm.then_inc(scores_ready, 1)

            def first_layer(i, tail):
                def probs(j, h):
                    return slot(j * HEADS + h)

                def times_v(j, half):
                    if j:
                        pe.wait_ge(u_saved, i * NT * NH + (j - 1) * NH + half + 1)
                    elif half == 0:
                        pe.wait_ge(v_ready, i + 1)
                        if tail:
                            pe.wait_ge(h1_ready, i)
                    s = slice(half * HALF, (half + 1) * HALF)
                    for h in range(HEADS):
                        d = slice(h * DH, (h + 1) * DH)
                        mm = pe.matmul(ps_u[d, s], v_sb[:, j, d], probs(j, h)[:, s], start=True, stop=True)
                    mm.then_inc(u_ready, 1)

                def sums(j, quarters):
                    if quarters[0] == 0:
                        pe.wait_ge(probs_ready, i * NT * HEADS + (j + 1) * HEADS)
                    for c in quarters:
                        k = j * Q + c
                        for h in range(HEADS):
                            mm = pe.matmul(chunk_sums[j >= CUT][h * DH:(h + 1) * DH, :],
                                           one_hot[:, DH - 1 - k:2 * DH - 1 - k],
                                           probs(j, h)[:, c * NQ:(c + 1) * NQ],
                                           start=(k in (0, CUT * Q)), stop=(k in (CUT * Q - 1, NT * Q - 1)),
                                           skip_group_check=True)
                    if k in (CUT * Q - 1, NT * Q - 1):
                        mm.then_inc(sums_done, 1)

                for g in range(EARLY if tail else 0, NT * HEADS + HEADS + LAG, 2):
                    if g < NT * HEADS:
                        for n in (g, g + 1):
                            scores(i, n // HEADS, n % HEADS, tail)
                    if tail and g in TAIL_PE:
                        second_end(i - 1, TAIL_PE[g])
                    for n in HELD[g] if tail and g in HELD else (g, g + 1):
                        j, piece = divmod(n - HEADS - LAG, HEADS)
                        if j == NT - 1 and piece % 2 == 0:
                            if piece == 0:
                                pe.wait_ge(r_split, i * 2 + 1)
                                pe.wait_ge(exp_ready, (i + 1) * NT * HEADS)
                                for k in range(3):
                                    inverse_sums(i, k)
                            else:
                                inverse_sums(i, 3)
                        if j >= 0 and piece < 2:
                            sums(j, (2 * piece, 2 * piece + 1))
                        elif j >= 0:
                            times_v(j, piece - 2)

            def inverse_sums(i, j):
                if j == 0:
                    pe.wait_ge(sel_ready, 1)
                if j == CUT:
                    pe.wait_ge(r_split, i * 2 + 2)
                if j >= 2:
                    pe.wait_ge(u_scaled, i * NT + j - 1)
                for c in range(Q):
                    for n in range(2):
                        mm = pe.matmul(ps[j % 2][:, c * NQ:(c + 1) * NQ], sel[:, j * Q + c, :],
                                       r_part[:, int(j >= CUT), n, :], start=(n == 0), stop=(n == 1))
                mm.then_inc(r_ps, 1)

            def layers(i, last):
                def project(n, half):
                    j = GROUPS[n][-1]
                    final = n == len(GROUPS) - 1
                    if half == 0 and n == 0:
                        pe.wait_ge(u_saved, (i + 1) * NT * NH)
                    if half == 0 or final:
                        pe.wait_ge(added, i * ADDS + adds_before(j + 1) + (half if final else 0))
                    for t in range(half * NT // 2, (half + 1) * NT // 2):
                        mm = pe.matmul(ps_u[:, t * P:(t + 1) * P], parts[n][:, t * P:(t + 1) * P],
                                       w_t[:, 3, :], start=(n == 0 and t == half * NT // 2),
                                       stop=final, skip_group_check=True)
                    if final:
                        mm.then_inc(o_ps, 1)

                for j in range(4, NT):
                    inverse_sums(i, j)
                    for n, half in ((n, half) for n in range(len(GROUPS) - 1) for half in range(2)):
                        if j == min(GROUPS[n][-1] + 3 + half, NT - 1):
                            project(n, half)
                project(len(GROUPS) - 1, 0)
                project(len(GROUPS) - 1, 1)
                if not last:
                    turn_x(i + 1)
                    queries_keys(i + 1)

                for half in range(NH):
                    pe.wait_ge(dst_ready, i * 2 + half + 1)
                    for t in range(half * NT // 2, (half + 1) * NT // 2):
                        mm = pe.transpose(ps_rest[:, t * P:(t + 1) * P],
                                          dst_col[:, t:t + 1].broadcast_to([P, P]), ident[:])
                mm.then_inc(drow_ps, 1)
                for half in range(NH):
                    pe.wait_ge((x1_ready, x1_more)[half], i + 1)
                    for t in range(half * NT // 2, (half + 1) * NT // 2):
                        mm = pe.transpose(ps_u[:, t * P:(t + 1) * P], x1[:, t, :], ident[:])
                    mm.then_inc(x1T_ps, 1)
                pe.wait_ge(wa_ready, 1)
                pe.wait_ge(x1T_ready, i * 2 + 2)
                for t in range(NT):
                    mm = pe.matmul(ps_u[:, 2 * t:2 * t + 2], x1T[:, t * P:(t + 1) * P], wa[:],
                                   start=True, stop=True)
                mm.then_inc(sd_ps, 1)
                if not last:
                    pe.wait_ge(lo_ready, i * 2 + 3)
                for t in range(NT):
                    mm = pe.matmul(ps[1][:, t * P:(t + 1) * P], x1T[:, t * P:(t + 1) * P], w1_nat[:],
                                   start=True, stop=True)
                mm.then_inc(wh_ps, 1)
                if not last:
                    pe.wait_ge(lo_ready, i * 2 + 4)
                pe.wait_ge(wh_ready, i + 1)
                for half in range(NH):
                    pe.wait_ge(m_ready, i * 2 + half + 1)
                    for n, dst in ((1, ps[0]), (0, ps[1])):
                        for t in MAX_TILES[half]:
                            mm = pe.transpose(dst[:, t * P:(t + 1) * P],
                                              u_cols[:, n, t:t + 1].broadcast_to([P, P]), ident[:])
                        if half or n:
                            mm.then_inc(mrow_ps, 1)
                if not last:
                    values(i + 1, ps_rest)

                def sums1(group):
                    if group == 0 and not last:
                        pe.wait_ge(v_ready, i + 2)
                    for half in range(NH):
                        s = slice(half * HALF, (half + 1) * HALF)
                        for c in range(4):
                            mm = pe.matmul((ps_sum, ps_small)[half][c * DH:(c + 1) * DH, :], ones32[:],
                                           p_sb[:, 4 * group + c, s], start=(group == 0),
                                           stop=(group == 1), skip_group_check=True)
                    mm.then_inc(h_ps, 1)

                for t in range(NT):
                    if t >= NT - 3 and not last:
                        scores(i + 1, 0, t - NT + 3, True)
                    pe.wait_ge(probs1_ready, i * NT + t + 1)
                    for half in range(NH):
                        s = slice(half * HALF, (half + 1) * HALF)
                        pe.matmul(ps_u[:, s], wh[:, t * P:(t + 1) * P], p_sb[:, t, s],
                                  start=(t == 0), stop=(t == NT - 1), skip_group_check=True)
                    if t == 3:
                        sums1(0)
                if not last:
                    for g in range(3, EARLY):
                        scores(i + 1, 0, g, True)
                sums1(1)

            def second_end(i, step):
                if step == "den":
                    pe.wait_ge(den_ready, i * 2 + 2)
                    for t in range(NT):
                        mm = pe.matmul(ps_small[:, t:t + 1], den_sb[:, t * P:(t + 1) * P], quad_first[:],
                                       start=True, stop=True)
                    mm.then_inc(den_ps, 1)
                elif step == "turn":
                    pe.wait_ge(hT_ready, i + 1)
                    for t in range(NT):
                        mm = pe.transpose(ps_u[:, t * P:(t + 1) * P], hT[:, t * P:(t + 1) * P], ident[:])
                    mm.then_inc(hp_ps, 1)

            def turn_adj(t):
                pe.wait_ge(adj_cmp, 3 * t + 2)
                for m in range(2):
                    if t:
                        if m == 0:
                            pe.wait_ge(clip_made, t)
                        else:
                            made = [n for n in range(t) if (n in DVE_KEEPS) == (t - 1 in DVE_KEEPS)]
                            pe.wait_ge(keep_dve if t - 1 in DVE_KEEPS else keep_act, len(made))
                    for c in range(NT):
                        mm = pe.transpose(adj_t(m, t)[:, c * P:(c + 1) * P],
                                          adj_bf[t % 2][m][:, c * P:(c + 1) * P], ident_bf[:])
                    mm.then_inc(adj_ps, 1)

            turn_x(0)
            turn_adj(0)
            pe.wait_ge(wT_ready, 2)
            queries_keys(0)
            values(0, ps_u)
            for t in range(1, NT):
                turn_adj(t)
            pe.wait_ge(clip_made, NT)
            pe.wait_ge(keep_act, NT - len(DVE_KEEPS))
            pe.wait_ge(keep_dve, len(DVE_KEEPS))
            pe.wait_ge(b_loaded, 7 * 16)
            pe.wait_ge(out_stored, 16)
            pe.matmul(ps_small[:, 0:2], w1_t, a_sb[:], start=True, stop=True)
            pe.matmul(ps_small[:, P:2 * P], bias_col[:, 2:3].broadcast_to([P, P]), w_t[:, 3, :],
                      start=True, stop=True)
            pe.matmul(ps_small[:, 2 * P:3 * P], a_sb[:, 1:2].broadcast_to([P, P]), w1_t,
                      start=True, stop=True).then_inc(wa_ps, 1)
            pe.wait_ge(consts, 5 + HEADS)
            first_layer(0, False)
            with pe.Fori(0, B - 1) as i:
                layers(i, False)
                first_layer(i + 1, True)
            layers(B - 1, True)
            for step in TAIL_PE.values():
                second_end(B - 1, step)

        @block.vector
        def _(dve):
            def low_parts(i, which=(0, 1)):
                for n, (src, hi, lo) in enumerate(((ps[1], q_hi, q_lo), (ps[0], k_hi, k_lo))):
                    if n not in which:
                        continue
                    dve.wait_ge(hi_ready, i * 2 + n + 1)
                    dve.scalar_tensor_tensor(out=lo, in0=src[:], scalar=bias_col[:, n:n + 1],
                                             in1=hi.bitcast(F32), op0=ALU.add, op1=ALU.subtract
                                             ).then_inc(lo_ready, 1)

            def tiles(ap):
                return ap.rearrange("p (t f) -> p t f", f=F)

            HALF_TILES = (range(0, NT // 2), range(NT // 2, NT))

            def invert(i, part):
                steps = [i * 6 + part * 3]

                def chain(ins):
                    steps[0] = steps[0] + 1
                    ins.then_inc(r_chain, 1)
                    dve.wait_ge(r_chain, steps[0])

                dve.wait_ge(sums_done, i * 2 + part + 1)
                chain(dve.tensor_scalar(r_sb[:], chunk_sums[part], TINY, None, ALU.max))
                chain(dve.reciprocal(r_sb[:], r_sb[:]))
                chain(dve.tensor_copy(r_part[:, part, 0, :], r_sb[:]))
                dve.tensor_tensor(r_part[:, part, 1, :], r_sb[:], r_part[:, part, 0, :].bitcast(F32),
                                  ALU.subtract).then_inc(r_split, 1)

            def first_layer(i, end):
                for g in range(NT * HEADS):
                    j = g // HEADS
                    if g == (CUT + 1) * HEADS:
                        invert(i, 0)
                    dve.wait_ge(exp_ready, i * NT * HEADS + g + 1)
                    dve.scalar_tensor_tensor(out=slot(g), in0=slot(g), scalar=LO, in1=clip_t[:, j, :],
                                             op0=ALU.max, op1=ALU.min).then_inc(probs_ready, 1)
                    if end and g in TAIL_DVE:
                        end(TAIL_DVE[g])

            def layers(i, last):
                steps = [0]

                def mark(ins):
                    steps[0] += 1
                    ins.then_inc(dve_chain, 1)
                    return steps[0]

                def need(step):
                    dve.wait_ge(dve_chain, i * DVE_CHAIN + step)

                def chain(ins):
                    need(mark(ins))

                def take_stats(src, which):
                    for t in which:
                        ins = dve.bn_stats(stats[:, t, :], src[:, t, :])
                    return ins

                def variance():
                    dve.tensor_tensor(halves[:, 0, :], stats[:, :, 1], stats[:, :, 4], ALU.add)
                    step = mark(dve.tensor_tensor(halves[:, 1, :], stats[:, :, 1], stats[:, :, 4],
                                                  ALU.subtract))
                    dve.tensor_tensor(halves[:, 2, :], stats[:, :, 2], stats[:, :, 5], ALU.add)
                    need(step)
                    dve.tensor_tensor(halves[:, 3, :], halves[:, 1, :], halves[:, 1, :], ALU.mult)
                    chain(dve.tensor_scalar(mean[:], halves[:, 0, :], 0.5, None, ALU.mult))
                    dve.scalar_tensor_tensor(out=f_var[:], in0=halves[:, 3, :], scalar=F / 4,
                                             in1=halves[:, 2, :], op0=ALU.mult, op1=ALU.add
                                             ).then_inc(var_ready, 1)

                def normalise(src, dst, which):
                    for t in which:
                        ins = dve.tensor_scalar(dst[:, t, :], src[:, t, :], mean[:, t:t + 1],
                                                rstd_col[:, t:t + 1], ALU.subtract, ALU.mult)
                    return ins

                starts = {g[0]: n for n, g in enumerate(GROUPS)}
                group_of = {j: n for n, g in enumerate(GROUPS) for j in g}

                def add(j):
                    n = group_of[j]
                    dve.wait_ge(u_scaled, i * NT + j + 1)
                    if j - 1 not in starts:
                        dve.wait_ge(added, i * ADDS + adds_before(j))
                    for s in (slice(0, N),) if j < NT - 1 else (slice(0, HALF), slice(HALF, N)):
                        dve.tensor_tensor(parts[n][:, s], parts[n][:, s], u_sb[:, j, s], ALU.add
                                          ).then_inc(added, 1)

                for j in range(NT):
                    if j == 3:
                        invert(i, 1)
                    dve.wait_ge(u_saved, i * NT * NH + (j + 1) * NH)
                    dve.wait_ge(r_ps, i * NT + j + 1)
                    dst = parts[starts[j]] if j in starts else u_sb[:, j, :]
                    dve.tensor_tensor(dst, u_sb[:, j, :], ps[j % 2][:], ALU.mult).then_inc(u_scaled, 1)
                    if j and j - 1 not in starts:
                        add(j - 1)
                add(NT - 1)
                dve.wait_ge(xb_ready, i * 2 + 2)
                for half in range(NH):
                    s = slice(half * HALF, (half + 1) * HALF)
                    dve.wait_ge(o_ps, i * 2 + half + 1)
                    step = mark(dve.tensor_tensor(y0[:, s], ps_u[:, s], xb[:, s], ALU.add))
                    if half:
                        take_stats(tiles(y0), HALF_TILES[0])
                    else:
                        first = step
                        need(first)
                need(step)
                chain(take_stats(tiles(y0), HALF_TILES[1]))
                variance()
                for t in range(NT):
                    ins = dve.scalar_tensor_tensor(out=tiles(g0)[:, t, :], in0=tiles(y0)[:, t, :],
                                                   scalar=mean[:, t:t + 1], in1=rows[:, 1, :],
                                                   op0=ALU.subtract, op1=ALU.mult)
                chain(ins)
                dve.wait_ge(rstd_ready, i * 3 + 1)
                done = []
                for which in HALF_TILES:
                    for t in which:
                        ins = dve.scalar_tensor_tensor(out=tiles(z0)[:, t, :], in0=tiles(g0)[:, t, :],
                                                       scalar=rstd_col[:, t:t + 1],
                                                       in1=tiles(x_beta)[:, t, :],
                                                       op0=ALU.mult, op1=ALU.add)
                    done.append(mark(ins))
                need(done[0])
                take_stats(tiles(z0), HALF_TILES[0])
                need(done[1])
                chain(take_stats(tiles(z0), HALF_TILES[1]))
                variance()
                if not last:
                    low_parts(i + 1, (0,))
                dve.wait_ge(rstd_ready, i * 3 + 2)
                dve.scalar_tensor_tensor(out=shift_col[:], in0=mean[:], scalar=-1.0, in1=rstd_col[:],
                                         op0=ALU.mult, op1=ALU.mult).then_inc(shift_ready, 1)
                normalise(tiles(z0), x1, HALF_TILES[0]).then_inc(x1_ready, 1)
                for half, (which, done) in enumerate(zip(HALF_TILES, (x1_ready, x1_more))):
                    if half == 0:
                        dve.wait_ge(wa_ready, 2)
                    dve.wait_ge(done, i + 1)
                    dve.memset(m_col[:, half:half + 1], 0.0)
                    for t in which:
                        ins = dve.tensor_tensor_reduce(parts[1][:, t * P:(t + 1) * P], x1[:, t, :],
                                                       wa_row[:], 1.0, 0.0, ALU.mult, ALU.add,
                                                       dst_col[:, t:t + 1])
                    ins.then_inc(dst_ready, 1)
                if not last:
                    low_parts(i + 1, (1,))
                dve.wait_ge(drow_ps, i + 1)
                dve.memset(m_col[:, 2:3], 0.0)
                for half, which in enumerate(MAX_TILES):
                    w = slice(which[0], which[-1] + 1)
                    for t in which:
                        ins = dve.tensor_tensor_reduce(p_sb[:, t, :], ps_rest[:], bias_n[:, t, :], 1.0,
                                                       NEG_BIG, ALU.add, ALU.max, row_max[:, t:t + 1])
                    if half == 0:
                        dve.wait_ge(sd_ps, i + 1)
                        ins = dve.tensor_copy(sd_col[:].rearrange("p t c -> p (t c)"), ps_u[:, 0:2 * NT])
                    chain(ins)
                    step = mark(dve.tensor_tensor(m_tmp[:, w], row_max[:, w], sd_col[:, w, 0], ALU.add))
                    dve.tensor_scalar(d_slope[:, w], sd_col[:, w, 1], NEG_SLOPE, None, ALU.mult)
                    need(step)
                    chain(dve.scalar_tensor_tensor(out=m_col[:, w], in0=m_tmp[:, w], scalar=NEG_SLOPE,
                                                   in1=m_tmp[:, w], op0=ALU.mult, op1=ALU.max))
                    dve.tensor_tensor(u_cols[:, 0, w], sd_col[:, w, 0], m_col[:, w], ALU.subtract)
                    dve.scalar_tensor_tensor(out=u_cols[:, 1, w], in0=sd_col[:, w, 0], scalar=NEG_SLOPE,
                                             in1=m_col[:, w], op0=ALU.mult, op1=ALU.subtract
                                             ).then_inc(m_ready, 1)
                dve.wait_ge(mrow_ps, i * 3 + 3)

                def mask1(t):
                    dve.wait_ge(exp1_ready, i * NT + t + 1)
                    dve.tensor_tensor(p_sb[:, t, :], e_sb[:, t % E_SLOTS, :], keep_t[:, t, :], ALU.min
                                      ).then_inc(probs1_ready, 1)

                for t in range(NT):
                    dve.wait_ge(slope_ready, i * NT + t + 1)
                    dve.scalar_tensor_tensor(out=e_sb[:, t % E_SLOTS, :], in0=ps[1][:],
                                             scalar=sd_col[:, t, 1:2], in1=e_sb[:, t % E_SLOTS, :],
                                             op0=ALU.add, op1=ALU.max).then_inc(shifted, 1)
                    if t:
                        mask1(t - 1)
                mask1(NT - 1)

                left = {}

                def end(step):
                    if step == "den":
                        dve.wait_ge(h_ps, i * 2 + 2)
                        dve.tensor_copy(den_sb[:, 0:HALF], ps_sum).then_inc(den_ready, 1)
                        dve.tensor_copy(den_sb[:, HALF:N], ps_small).then_inc(den_ready, 1)
                    elif step == "inverse":
                        dve.wait_ge(den_ps, i + 1)
                        dve.reciprocal(den[:], ps_small[:, 0:NT]).then_inc(den_inv, 1)
                    elif step == "residual":
                        dve.wait_ge(h1_ready, i + 1)
                        left["z1"] = mark(dve.scalar_tensor_tensor(
                            out=tiles(z1), in0=tiles(h1), scalar=0.0, in1=x1[:], op0=ALU.max,
                            op1=ALU.add))
                    elif step == "elu":
                        need(left["z1"])
                        dve.wait_ge(elu_exp, i + 1)
                        left["h1"] = mark(dve.scalar_tensor_tensor(
                            out=h1, in0=h_exp, scalar=-1.0, in1=z1, op0=ALU.add, op1=ALU.add))
                    elif step == "stats0":
                        need(left["h1"])
                        take_stats(tiles(h1), HALF_TILES[0])
                    elif step == "stats1":
                        left["stats"] = mark(take_stats(tiles(h1), HALF_TILES[1]))
                    elif step == "variance":
                        need(left["stats"])
                        variance()
                    elif step == "out0":
                        dve.wait_ge(rstd_ready, i * 3 + 3)
                        normalise(tiles(h1), tiles(out_sb), HALF_TILES[0])
                    elif step == "out1":
                        normalise(tiles(h1), tiles(out_sb), HALF_TILES[1]).then_inc(out_ready, 1)
                        assert steps[0] == DVE_CHAIN, steps
                return end

            for t in range(NT):
                if t == 2:
                    dve.wait_ge(b_loaded, 7 * 16)
                    low_parts(0)
                dve.wait_ge(adj_loaded[t], 16)
                if t >= 2:
                    dve.wait_ge(adj_ps, 2 * (t - 1))
                nonzero, positive = adj_bf[t % 2]
                dve.tensor_scalar(nonzero, adj_i[t], 0.0, None, ALU.not_equal).then_inc(adj_cmp, 1)
                dve.tensor_scalar(positive, adj_i[t], 0.0, None, ALU.is_gt).then_inc(adj_cmp, 1)
                dve.wait_ge(adj_cmp, 3 * t + 2)
                dve.tensor_scalar(bias_n[:, t, :], positive, -1.0, -NEG_BIG, ALU.add, ALU.mult
                                  ).then_inc(adj_cmp, 1)
                if t - 1 in DVE_KEEPS:
                    dve.wait_ge(adj_ps, 2 * t)
                    dve.tensor_scalar(keep_t[:, :, (t - 1) * P:t * P],
                                      adj_t(1, t - 1).rearrange("p (c q) -> p c q", q=P), 255.0, None,
                                      ALU.mult).then_inc(keep_dve, 1)
            dve.wait_ge(adj_cmp, 3 * NT)
            dve.wait_ge(wa_ps, 1)
            dve.tensor_copy(wa[:], ps_small[:, 0:2]).then_inc(wa_ready, 1)
            dve.tensor_copy(wa_row[:], ps_small[:, 2 * P:3 * P]).then_inc(wa_ready, 1)
            dve.scalar_tensor_tensor(out=rows[:, 0, :], in0=ps_small[:, P:2 * P], scalar=float(NT),
                                     in1=rows[:, 0, :], op0=ALU.mult, op1=ALU.add).then_inc(bo_ready, 1)
            first_layer(0, None)
            with dve.Fori(0, B - 1) as i:
                first_layer(i + 1, layers(i, False))
            end = layers(B - 1, True)
            for step in TAIL_DVE.values():
                end(step)


_INS = ["x", "adj", "L0_gnn_Wq", "L0_gnn_bq", "L0_gnn_Wk", "L0_gnn_bk", "L0_gnn_Wv", "L0_gnn_bv",
        "L0_gnn_Wo", "L0_gnn_bo", "L0_gnn_gamma", "L0_gnn_beta", "L1_gnn_W", "L1_gnn_a"]


def kernel(**inputs):
    import numpy as _np
    import concourse.bacc as _bacc
    from concourse import mybir as _mybir
    from concourse.bass_utils import run_bass_kernel_spmd as _run

    nc = _bacc.Bacc("TRN2", target_bir_lowering=False, num_devices=1)
    arrays, args = {}, []
    for name in _INS:
        a = _np.ascontiguousarray(inputs[name])
        arrays[f"in_{name}"] = a
        args.append(nc.dram_tensor(f"in_{name}", a.shape, _mybir.dt.from_np(a.dtype),
                                   kind="ExternalInput").ap())
    shape = tuple(inputs["x"].shape)
    args.append(nc.dram_tensor("out_dram", shape, _mybir.dt.from_np(_np.dtype("float32")),
                               kind="ExternalOutput").ap())
    build(nc, *args)
    r = _run(nc, [arrays], core_ids=[0])
    return r.results[0]["out_dram"]
```
